# Optimizing a Trainium2 kernel written in Bass

```python
import numpy as np
import jax
import jax.numpy as jnp

def _softmax(x, axis=-1):
    return jax.nn.softmax(x, axis=axis)

def _gelu(x):
    return jax.nn.gelu(x, approximate=True)

def _silu(x):
    return jax.nn.silu(x)

def _sigmoid(x):
    return jax.nn.sigmoid(x)

def _layernorm(x, axis=-1, eps=1e-05):
    m = jnp.mean(x, axis=axis, keepdims=True)
    v = jnp.var(x, axis=axis, keepdims=True)
    return (x - m) / jnp.sqrt(v + eps)

def _scatter_add(tgt, idx, src, axis=0):
    return tgt.at[idx].add(src)

def _segment_sum(src, seg, n):
    return jax.ops.segment_sum(src, seg, n)
kernel_name = 'mk_gnn_resnorm_d2_gnn_r8_50df99'

def setup_inputs(seed: int=0):
    np.random.seed(seed)
    _w = jnp.asarray

    def _rec_inputs():
        import jax
        import jax.numpy as jnp
        _gk = jax.random.key(seed)
        x = -0.0003713 + 1 * jax.random.normal(jax.random.fold_in(_gk, 1), (12500, 128), jnp.float32)
        src = jax.random.randint(jax.random.fold_in(_gk, 2), (200000,), 0, 12500, jnp.int32)
        dst = jnp.minimum((12500 * jax.random.uniform(jax.random.fold_in(_gk, 3), (200000,)) ** 2.0).astype(jnp.int32), 99999)
        _o = jnp.argsort(dst, stable=True)
        src = src[_o]
        dst = dst[_o]
        edge_attr_128 = -5.16925e-05 + 1.00005 * jax.random.normal(jax.random.fold_in(_gk, 13), (200000, 128), jnp.float32)
        edge_weight = jax.random.uniform(jax.random.fold_in(_gk, 15), (200000,), jnp.float32, 0.0, 1)
        return (x, src, dst, edge_attr_128, edge_weight)
    x, src, dst, edge_attr_128, edge_weight = _rec_inputs()

    def _L0_gnn_setup():
        import jax, jax.numpy as jnp
        import numpy as np
        N_NODES = 12500
        N_EDGES = 400000
        D_IN = 128
        UNITS = 128
        key = jax.random.key(seed)
        k1, k2, k3, k4, k5, k6 = jax.random.split(key, 6)
        x = jax.random.normal(k1, (N_NODES, D_IN), dtype=jnp.float32)
        edge_src = jax.random.randint(k2, (N_EDGES,), 0, N_NODES, dtype=jnp.int32)
        edge_dst = jax.random.randint(k3, (N_EDGES,), 0, N_NODES, dtype=jnp.int32)
        edge_vals = jax.random.uniform(k4, (N_EDGES,), dtype=jnp.float32)
        w = jax.random.normal(k5, (D_IN, UNITS), dtype=jnp.float32) * (2.0 / D_IN) ** 0.5
        b = jax.random.normal(k6, (UNITS,), dtype=jnp.float32) * 0.05
        return {'x': x, 'edge_src': edge_src, 'edge_dst': edge_dst, 'edge_vals': edge_vals, 'w': w, 'b': b}
    _L0_gnn_all = _L0_gnn_setup()
    _L0_gnn_in = {k: v for k, v in _L0_gnn_all.items() if k in ('w', 'b')}
    del _L0_gnn_all

    def _L1_gnn_setup():
        import jax, jax.numpy as jnp
        import numpy as np
        N = 6250
        E = 100000
        NODE_DIM = 128
        EDGE_DIM = 128
        HIDDEN_DIM = 256
        key = jax.random.key(seed)
        k_x, k_ei, k_ea, k_w1, k_b1, k_w2, k_b2 = jax.random.split(key, 7)
        x = jax.random.normal(k_x, (N, NODE_DIM), dtype=jnp.float32)
        edge_index = jax.random.randint(k_ei, (2, E), 0, N, dtype=jnp.int64)
        edge_attr = jax.random.normal(k_ea, (E, EDGE_DIM), dtype=jnp.float32)
        u = jnp.zeros((1, NODE_DIM), dtype=jnp.float32)
        batch = jnp.zeros((N,), dtype=jnp.int64)
        in_dim = NODE_DIM + EDGE_DIM
        W1 = jax.random.normal(k_w1, (HIDDEN_DIM, in_dim), dtype=jnp.float32) / np.sqrt(in_dim)
        b1 = jax.random.normal(k_b1, (HIDDEN_DIM,), dtype=jnp.float32) * 0.01
        W2 = jax.random.normal(k_w2, (NODE_DIM, HIDDEN_DIM), dtype=jnp.float32) / np.sqrt(HIDDEN_DIM)
        b2 = jax.random.normal(k_b2, (NODE_DIM,), dtype=jnp.float32) * 0.01
        return {'x': x, 'edge_index': edge_index, 'edge_attr': edge_attr, 'u': u, 'batch': batch, 'W1': W1, 'b1': b1, 'W2': W2, 'b2': b2}
    _L1_gnn_all = _L1_gnn_setup()
    _L1_gnn_in = {k: v for k, v in _L1_gnn_all.items() if k in ('u', 'W1', 'b1', 'W2', 'b2')}
    del _L1_gnn_all
    return {'x': x, 'src': src, 'dst': dst, 'edge_attr_128': edge_attr_128, 'edge_weight': edge_weight, 'L0_gnn_w': _L0_gnn_in['w'], 'L0_gnn_b': _L0_gnn_in['b'], 'L1_gnn_u': _L1_gnn_in['u'], 'L1_gnn_W1': _L1_gnn_in['W1'], 'L1_gnn_b1': _L1_gnn_in['b1'], 'L1_gnn_W2': _L1_gnn_in['W2'], 'L1_gnn_b2': _L1_gnn_in['b2']}

def reference(x, src, dst, edge_attr_128, edge_weight, L0_gnn_w, L0_gnn_b, L1_gnn_u, L1_gnn_W1, L1_gnn_b1, L1_gnn_W2, L1_gnn_b2):
    import jax
    import jax.numpy as jnp

    def _L0_gnn_ref(x, edge_src, edge_dst, edge_vals, w, b):
        import jax, jax.numpy as jnp
        import numpy as np
        N_NODES = 12500
        N_EDGES = 400000
        D_IN = 128
        UNITS = 128
        h = x @ w
        msgs = edge_vals[:, None] * h[edge_src]
        agg = jax.ops.segment_sum(msgs, edge_dst, num_segments=N_NODES)
        return jax.nn.relu(agg + b)

    def _L1_gnn_ref(x, edge_index, edge_attr, u, batch, W1, b1, W2, b2):
        import jax, jax.numpy as jnp
        import numpy as np
        N = 6250
        E = 100000
        NODE_DIM = 128
        EDGE_DIM = 128
        HIDDEN_DIM = 256
        col = edge_index[1]
        agg = jax.ops.segment_sum(edge_attr, col, num_segments=x.shape[0])
        out = jnp.concatenate([x, agg], axis=1)
        h = jax.nn.relu(out @ W1.T + b1)
        return h @ W2.T + b2
    edge_index = jnp.stack([src, dst])
    batch0 = jnp.zeros((12500,), jnp.int32)
    x = _layernorm(x + _L0_gnn_ref(x, src, dst, edge_weight, L0_gnn_w, L0_gnn_b), axis=-1)
    x = _layernorm(x + _L1_gnn_ref(x, edge_index, edge_attr_128, L1_gnn_u, batch0, L1_gnn_W1, L1_gnn_b1, L1_gnn_W2, L1_gnn_b2), axis=-1)
    return x

_drawn_inputs = setup_inputs


def setup_inputs(seed=0):
    import zlib

    import numpy as np

    out = dict(_drawn_inputs(seed))
    spreads = {'L1_gnn_u': (0.0, 0.1)}
    factors = {'L0_gnn_b': 4.327, 'L1_gnn_b1': 8.0, 'L1_gnn_b2': 8.0}
    for name, (base, spread) in spreads.items():
        noise = np.random.default_rng([zlib.crc32(name.encode()), seed]).standard_normal(out[name].shape)
        drawn = base * np.exp(spread * noise) if base else spread * noise
        out[name] = jnp.asarray(drawn.astype(out[name].dtype))
    for name, factor in factors.items():
        out[name] = (out[name] * factor).astype(out[name].dtype)
    return out
```

```python
from contextlib import ExitStack

import numpy as np

import concourse.bass as bass
from concourse import mybir

F32 = mybir.dt.float32
I32 = mybir.dt.int32
ALU = mybir.AluOpType
ACT = mybir.ActivationFunctionType
AX = mybir.AxisListType

P = 128
SLOTS = 4
GROUP = P * SLOTS
WINDOW = 128
WIDE = 256
RING = 6
PAIRS = RING // 2
EPS = 1e-5


def wait(engine, semaphore, count):
    if not isinstance(count, int) or count > 0:
        engine.wait_ge(semaphore, count)


def wait_apart(engine, semaphore, count, waited):
    engine.wait_ge(semaphore, count)
    engine.sem_inc(waited, 1)


def build(nc, x, src, src_tail, dst, dst_tail, weight, weight_tail, attr, w0, b0, w1, b1, w2, b2, out):
    N, D = x.shape
    E = attr.shape[0]
    HID = b1.shape[0] * b1.shape[1]
    HALVES = HID // P
    assert D == P and HALVES == 2
    FULL = E // GROUP
    TAIL = (E - FULL * GROUP) // SLOTS
    NG = FULL + 1
    TURNS = FULL // RING
    assert FULL % RING == 0 and 0 < TAIL < P and TAIL * SLOTS + FULL * GROUP == E and NG <= 512
    NPAIR = FULL // 2
    BLOCKS = N // P
    LAST = N - BLOCKS * P
    assert 0 < LAST < P
    WINDOWS = -(-N // WIDE)
    SUMS = max(WINDOWS * WIDE, N - 1 + WINDOW, (BLOCKS + 1) * P)
    SUMS += SUMS % 2
    CH = -(-NG // P)
    LASTCH = NG - (CH - 1) * P

    ctx = ExitStack()
    with ctx:
        def sbuf(name, shape, dtype=F32):
            return ctx.enter_context(nc.sbuf_tensor(name, shape, dtype))

        def psum(name, shape):
            return ctx.enter_context(nc.psum_tensor(name, shape, F32))

        def sem(name):
            return ctx.enter_context(nc.semaphore(name))

        sums = sbuf("sums", [P, 2, SUMS])
        src_sb = sbuf("src_sb", [P, NG * SLOTS], I32)
        dst_i = sbuf("dst_i", [P, NG * SLOTS], I32)
        dst_f = sbuf("dst_f", [P, NG * SLOTS])
        local = sbuf("local", [P, NG * SLOTS])
        weight_sb = sbuf("weight_sb", [P, NG * SLOTS])
        attr_sb = sbuf("attr_sb", [P, PAIRS, 2, SLOTS, D])
        rows = sbuf("rows", [P, RING, SLOTS, D])
        staged = sbuf("staged", [P, RING, SLOTS], I32)
        onehot = sbuf("onehot", [P, 2, SLOTS, 2, WINDOW])
        wide_onehot = onehot[:, :, :, :, :].rearrange("p a s k w -> p (a s k w)").rearrange(
            "p (s k w) -> p s k w", s=SLOTS, k=2)
        ident = sbuf("ident", [P, P])
        ones = sbuf("ones", [P, P])
        zero = sbuf("zero", [P, 1])
        eps = sbuf("eps", [P, 1])
        iota_i = sbuf("iota_i", [P, WIDE], I32)
        iota = sbuf("iota", [P, WIDE])
        w0_sb = sbuf("w0_sb", [P, D])
        b0_sb = sbuf("b0_sb", [P, 1])
        w1_sb = sbuf("w1_sb", [P, 2, HID])
        b1_sb = sbuf("b1_sb", [P, HALVES])
        w2_sb = sbuf("w2_sb", [P, HALVES, D])
        b2_sb = sbuf("b2_sb", [1, D])
        ends = sbuf("ends", [P, 2, NG])
        ends_t = sbuf("ends_t", [P, 2, CH])
        diag = sbuf("diag", [P, 2, CH, P])
        base_f = sbuf("base_f", [P, NG])
        base_i = sbuf("base_i", [1, NG], I32)
        span = sbuf("span", [P, NG])
        any_wide = sbuf("any_wide", [P, 3])
        wide_i = sbuf("wide_i", [1, 1], I32)
        later = sbuf("later", [1, 2, NG])
        ready_i = sbuf("ready_i", [1, NPAIR], I32)
        ready = sbuf("ready", [1, NPAIR])
        done = sbuf("done", [1, NPAIR + 1])
        table = sbuf("table", [1, NPAIR + 1, 2], I32)
        relative = sbuf("relative", [P, SLOTS])
        x_sb = sbuf("x_sb", [P, D])
        r0T = sbuf("r0T", [P, P])
        s1 = sbuf("s1", [P, D])
        x1 = sbuf("x1", [P, D])
        x1T = sbuf("x1T", [P, P])
        hT = sbuf("hT", [P, HALVES, P])
        s2 = sbuf("s2", [P, D])
        x2 = sbuf("x2", [P, D])
        stats = sbuf("stats", [P, 2, 6])
        moments = sbuf("moments", [P, 2, 2])
        deviation = sbuf("deviation", [P, 2, 2])

        group_ps = [psum(f"group_ps{i}", [P, 2, WIDE]) for i in range(2)]
        z0_ps = psum("z0_ps", [P, 512])
        r0_ps = psum("r0_ps", [P, 512])
        x1T_ps = psum("x1T_ps", [P, 512])
        h_ps = [psum(f"h_ps{k}", [P, 512]) for k in range(HALVES)]
        y_ps = psum("y_ps", [P, 512])
        ends_ps = y_ps

        src_loaded = sem("src_loaded")
        dst_loaded = sem("dst_loaded")
        weight_loaded = sem("weight_loaded")
        params_loaded = sem("params_loaded")
        attr_loaded = [sem(f"attr_loaded{i}") for i in range(PAIRS)]
        gathered = [sem(f"gathered{i}") for i in range(RING)]
        consts_zeroed = sem("consts_zeroed")
        consts_ready = sem("consts_ready")
        zero_ready = sem("zero_ready")
        sums_zeroed = sem("sums_zeroed")
        setup_step = sem("setup_step")
        ends_ready = sem("ends_ready")
        ends_transposed = sem("ends_transposed")
        ends_reduced = sem("ends_reduced")
        diag_ready = sem("diag_ready")
        ends_spread = sem("ends_spread")
        base_read = sem("base_read")
        tables_ready = sem("tables_ready")
        staged_ready = sem("staged_ready")
        onehot_ready = sem("onehot_ready")
        group_summed = sem("group_summed")
        sums_added = sem("sums_added")
        sums_final = sem("sums_final")
        wide_attr_loaded = sem("wide_attr_loaded")
        wide_staged = sem("wide_staged")
        wide_gathered = sem("wide_gathered")
        wide_step = sem("wide_step")
        wide_ready = sem("wide_ready")
        wide_summed = sem("wide_summed")
        wide_added = sem("wide_added")
        x_loaded = sem("x_loaded")
        z0_ready = sem("z0_ready")
        r0T_ready = sem("r0T_ready")
        r0_ready = sem("r0_ready")
        norm_step = sem("norm_step")
        moments_ready = sem("moments_ready")
        deviation_ready = sem("deviation_ready")
        x1_ready = sem("x1_ready")
        x1T_ready = sem("x1T_ready")
        x1T_copied = sem("x1T_copied")
        h_ready = sem("h_ready")
        hT_ready = sem("hT_ready")
        y_ready = sem("y_ready")
        x2_ready = sem("x2_ready")
        x2_stored = sem("x2_stored")
        pool_waited = sem("pool_waited")
        dve_waited = sem("dve_waited")
        pe_waited = sem("pe_waited")

        src_v = src_sb[:, :].rearrange("p (g s) -> p g s", s=SLOTS)
        dst_v = dst_f[:, :].rearrange("p (g s) -> p g s", s=SLOTS)
        local_v = local[:, :].rearrange("p (g s) -> p g s", s=SLOTS)
        attr_pairs = attr[0:FULL * GROUP, :].rearrange("(q a p s) d -> q p a (s d)", a=2, p=P, s=SLOTS)
        attr_groups = attr[0:FULL * GROUP, :].rearrange("(g p s) d -> g p (s d)", p=P, s=SLOTS)
        attr_tail = attr[FULL * GROUP:E, :].rearrange("(p s) d -> p (s d)", s=SLOTS)
        MAIN = FULL * SLOTS

        def block_turn(engine, q):
            go = engine.value_load(table[0:1, bass.ds(q, 1), 0:1].rearrange("a b c -> a (b c)"), min_val=0, max_val=1)
            b = engine.value_load(table[0:1, bass.ds(q, 1), 1:2].rearrange("a b c -> a (b c)"),
                                  min_val=0, max_val=BLOCKS - 1)
            return go, b

        def remaining(engine, body):
            first = engine.value_load(table[0:1, NPAIR, 1:2], min_val=0, max_val=BLOCKS - 1)
            with engine.Fori(first, BLOCKS) as b:
                body(b, P)
            body(BLOCKS, LAST)

        block = ctx.enter_context(nc.Block())

        @block.sync
        def _(sp):
            sp.dma_start(src_sb[:, 0:MAIN], src).then_inc(src_loaded, 16)
            sp.dma_start(src_sb[0:TAIL, MAIN:], src_tail).then_inc(src_loaded, 16)
            sp.dma_start(dst_i[:, 0:MAIN], dst).then_inc(dst_loaded, 16)
            sp.dma_start(dst_i[0:TAIL, MAIN:], dst_tail).then_inc(dst_loaded, 16)
            sp.dma_start(weight_sb[:, 0:MAIN], weight).then_inc(weight_loaded, 16)
            sp.dma_start(weight_sb[0:TAIL, MAIN:], weight_tail).then_inc(weight_loaded, 16)

            def load_attr(q, slot):
                sp.dma_start(attr_sb[:, slot, :, :, :].rearrange("p a s d -> p a (s d)"),
                             attr_pairs[bass.ds(q, 1), :, :, :].rearrange("q p a n -> (q p) a n")
                             if not isinstance(q, int) else attr_pairs[q]).then_inc(attr_loaded[slot], 16)

            for j in range(PAIRS):
                load_attr(j, j)
            for sb, dram in ((w0_sb[:, :], w0), (b0_sb[:, :], b0), (w1_sb[:, :, :], w1), (b1_sb[:, :], b1),
                             (w2_sb[:, :, :], w2), (b2_sb[:, :], b2)):
                sp.dma_start(sb, dram).then_inc(params_loaded, 16)

            def load_x(b, n):
                wait(sp, x1_ready, b)
                sp.dma_start(x_sb[0:n, :], x[bass.ds(b * P, n), :]).then_inc(x_loaded, 16)

            sp.wait_ge(tables_ready, 1)
            with sp.Fori(0, TURNS - 1) as t:
                for j in range(PAIRS):
                    q = t * PAIRS + j
                    go, b = block_turn(sp, q)
                    with sp.If(go > 0):
                        load_x(b, P)
                    sp.wait_ge(group_summed, 2 * q + 2)
                    load_attr(q + PAIRS, j)
            for j in range(PAIRS):
                go, b = block_turn(sp, NPAIR - PAIRS + j)
                with sp.If(go > 0):
                    load_x(b, P)
                if j == 0:
                    sp.wait_ge(group_summed, FULL - 2 * PAIRS + 2)
                    sp.dma_start(attr_sb[0:TAIL, 0, 0, :, :].rearrange("p s d -> p (s d)"),
                                 attr_tail).then_inc(attr_loaded[0], 16)

            wide = sp.value_load(wide_i[0:1, 0:1], min_val=0, max_val=1)
            with sp.If(wide > 0):
                sp.wait_ge(group_summed, NG)
                with sp.Fori(0, FULL) as g:
                    sp.wait_ge(wide_summed, g * WINDOWS)
                    sp.dma_start(attr_sb[:, 0, 0, :, :].rearrange("p s d -> p (s d)"),
                                 attr_groups[bass.ds(g, 1), :, :].rearrange("g p n -> (g p) n")
                                 ).then_inc(wide_attr_loaded, 16)
                sp.wait_ge(wide_summed, FULL * WINDOWS)
                sp.dma_start(attr_sb[0:TAIL, 0, 0, :, :].rearrange("p s d -> p (s d)"),
                             attr_tail).then_inc(wide_attr_loaded, 16)

            remaining(sp, load_x)
            sp.wait_ge(x2_stored, 16 * (BLOCKS + 1))

        @block.gpsimd
        def _(pool):
            pool.memset(zero[:, :], 0.0).then_inc(zero_ready, 1)
            pool.memset(ident[:, :], 0.0).then_inc(consts_zeroed, 1)
            pool.memset(ones[:, :], 1.0).then_inc(consts_ready, 1)
            pool.memset(eps[:, :], EPS).then_inc(consts_ready, 1)
            pool.iota(iota_i[:, :], pattern=[[1, WIDE]], base=0, channel_multiplier=0).then_inc(consts_ready, 1)
            pool.wait_ge(consts_zeroed, 1)
            pool.affine_select(out=ident[:, :], in_=ident[:, :], compare_op=ALU.not_equal, fill=1.0, base=0,
                               pattern=[[-1, P]], channel_multiplier=1).then_inc(consts_ready, 1)

            def gather(slot, n, semaphore):
                for s in range(SLOTS):
                    pool.indirect_dma_start(rows[0:n, slot, s, :], None, x,
                                            bass.IndirectOffsetOnAxis(ap=staged[0:n, slot, s:s + 1], axis=0)
                                            ).then_inc(semaphore, 16)

            with pool.Fori(0, TURNS) as t:
                for k in range(RING):
                    wait_apart(pool, staged_ready, t * RING + k + 1, pool_waited)
                    gather(k, P, gathered[k])
            pool.wait_ge(staged_ready, NG)
            gather(0, TAIL, gathered[0])

            pool.wait_ge(tables_ready, 1)
            wide = pool.value_load(wide_i[0:1, 0:1], min_val=0, max_val=1)
            with pool.If(wide > 0):
                with pool.Fori(0, FULL) as g:
                    wait_apart(pool, wide_staged, g + 1, pool_waited)
                    gather(0, P, wide_gathered)
                pool.wait_ge(wide_staged, NG)
                gather(0, TAIL, wide_gathered)

        @block.vector
        def _(dve):
            steps = [0]

            def step(instruction):
                steps[0] += 1
                instruction.then_inc(setup_step, 1)
                dve.wait_ge(setup_step, steps[0])

            def stage(g, slot, n=P):
                nc.vector.tensor_copy(staged[0:n, slot, :], src_sb[0:n, bass.ds(g * SLOTS, SLOTS)]
                                      ).then_inc(staged_ready, 1)

            dve.wait_ge(src_loaded, 32)
            for k in range(RING):
                stage(k, k)

            dve.wait_ge(dst_loaded, 32)
            nc.vector.tensor_copy(dst_f[:, 0:MAIN], dst_i[:, 0:MAIN])
            nc.vector.memset(ends[:, 0, FULL:NG], 3e4)
            nc.vector.memset(ends[:, 1, FULL:NG], -3e4)
            step(nc.vector.tensor_copy(dst_f[0:TAIL, MAIN:], dst_i[0:TAIL, MAIN:]))
            for k, op in enumerate((ALU.min, ALU.max)):
                nc.vector.tensor_reduce(ends[:, k, 0:FULL], dst_v[:, 0:FULL, :], axis=AX.X, op=op)
                nc.vector.tensor_reduce(ends[0:TAIL, k, FULL:NG], dst_v[0:TAIL, FULL:NG, :], axis=AX.X,
                                        op=op).then_inc(ends_ready, 1)
            dve.wait_ge(consts_ready, 4)
            nc.vector.tensor_copy(iota[:, :], iota_i[:, :])
            last = CH - 1
            for k, op in enumerate((ALU.min, ALU.max)):
                dve.wait_ge(ends_transposed, k + 1)
                view = ends_ps[:, :].rearrange("p (c e) -> p c e", e=P)
                if CH > 1:
                    nc.vector.tensor_reduce(ends_t[:, k, 0:last], view[:, 0:last, :], axis=AX.X, op=op)
                step(nc.vector.tensor_reduce(ends_t[0:LASTCH, k, last:CH], view[0:LASTCH, last:CH, :],
                                             axis=AX.X, op=op))
                for c in range(CH):
                    n = P if c < last else LASTCH
                    ins = nc.vector.tensor_scalar(diag[0:n, k, c, :], ident[0:n, :], ends_t[0:n, k, c:c + 1], None,
                                                  ALU.mult)
                ins.then_inc(ends_reduced, 1)
            dve.wait_ge(ends_spread, 1)
            step(nc.vector.tensor_copy(base_f[:, :], z0_ps[:, 0:NG]))
            for n, lo, hi in ((P, 0, FULL), (TAIL, FULL, NG)):
                nc.vector.tensor_tensor(local_v[0:n, lo:hi, :], dst_v[0:n, lo:hi, :],
                                        base_f[0:n, lo:hi].unsqueeze(2).to_broadcast([n, hi - lo, SLOTS]),
                                        ALU.subtract)
            step(nc.vector.tensor_copy(base_i[0:1, :], base_f[0:1, :]))
            dve.wait_ge(ends_spread, 2)
            step(nc.vector.tensor_tensor(span[:, :], r0_ps[:, 0:NG], base_f[:, :], ALU.subtract))
            step(nc.vector.tensor_reduce(any_wide[:, 0:1], span[:, :], axis=AX.X, op=ALU.max))
            step(nc.vector.tensor_scalar(any_wide[:, 1:2], any_wide[:, 0:1], float(WINDOW), None, ALU.is_ge))
            nc.vector.tensor_copy(wide_i[0:1, :], any_wide[0:1, 1:2])
            step(nc.vector.tensor_scalar(any_wide[:, 2:3], any_wide[:, 1:2], -1.0, 1.0, ALU.mult, ALU.add))
            step(nc.vector.tensor_copy(later[0:1, 0, :], base_f[0:1, :]))
            reach, k = 1, 0
            while reach < NG:
                nc.vector.tensor_copy(later[0:1, 1 - k, NG - reach:NG], later[0:1, k, NG - reach:NG])
                step(nc.vector.tensor_tensor(later[0:1, 1 - k, 0:NG - reach], later[0:1, k, 0:NG - reach],
                                             later[0:1, k, reach:NG], ALU.min))
                reach, k = 2 * reach, 1 - k
            step(nc.vector.tensor_copy(ready_i[0:1, 1:NPAIR], later[0:1, k, 1:2 * NPAIR - 2:2]))
            step(nc.vector.tensor_single_scalar(ready_i[0:1, 1:NPAIR], ready_i[0:1, 1:NPAIR],
                                                P.bit_length() - 1, ALU.arith_shift_right))
            step(nc.vector.tensor_copy(ready[0:1, 1:NPAIR], ready_i[0:1, 1:NPAIR]))
            step(nc.vector.tensor_scalar(ready[0:1, 1:NPAIR], ready[0:1, 1:NPAIR], any_wide[0:1, 2:3],
                                         float(BLOCKS - 1), ALU.mult, ALU.min))
            step(nc.vector.memset(ready[0:1, 0:PAIRS], 0.0))
            step(nc.vector.memset(done[0:1, 0:1], 0.0))
            step(nc.vector.tensor_tensor_scan(done[0:1, 1:NPAIR + 1], ones[0:1, 0:1].to_broadcast([1, NPAIR]),
                                              ready[0:1, :], 0.0, ALU.add, ALU.min))
            nc.vector.tensor_copy(table[0:1, :, 1:2].rearrange("a b c -> a (b c)"), done[0:1, :])
            nc.vector.tensor_tensor(table[0:1, 0:NPAIR, 0:1].rearrange("a b c -> a (b c)"), done[0:1, 1:NPAIR + 1],
                                    done[0:1, 0:NPAIR], ALU.subtract).then_inc(tables_ready, 1)
            dve.wait_ge(tables_ready, 1)
            dve.wait_ge(weight_loaded, 32)

            def make_onehots(g, slot, n=P):
                wait(dve, group_summed, g - 1)
                for s in range(SLOTS):
                    at = local[0:n, bass.ds(g * SLOTS + s, 1)]
                    nc.vector.tensor_scalar(onehot[0:n, slot, s, 1, :], iota[0:n, 0:WINDOW], at, None, ALU.is_equal)
                    ins = nc.vector.tensor_scalar(onehot[0:n, slot, s, 0, :], iota[0:n, 0:WINDOW], at,
                                                  weight_sb[0:n, bass.ds(g * SLOTS + s, 1)], ALU.is_equal, ALU.mult)
                ins.then_inc(onehot_ready, 1)

            def add_sums(g, slot):
                base = dve.value_load(base_i[0:1, bass.ds(g, 1)], min_val=0, max_val=N - 1)
                at = sums[:, :, bass.ds(base, WINDOW)]
                wait(dve, sums_added, g)
                dve.wait_ge(group_summed, g + 1)
                nc.vector.tensor_tensor(at, at, group_ps[slot][:, :, 0:WINDOW], ALU.add).then_inc(sums_added, 1)

            def norm_moments(layer, b, n, s):
                count = 6 * b + 3 * layer
                dve.wait_ge(norm_step, count + 1)
                nc.vector.bn_stats(stats[0:n, layer, :], s[0:n, :]).then_inc(norm_step, 1)
                wait_apart(dve, norm_step, count + 2, dve_waited)
                nc.vector.bn_aggr(moments[0:n, layer, :], stats[0:n, layer, :]).then_inc(moments_ready, 1)

            def normalise(layer, b, n, s, to, semaphore):
                count = 6 * b + 3 * layer
                dve.wait_ge(deviation_ready, 2 * b + layer + 1)
                nc.vector.reciprocal(deviation[0:n, layer, 1:2], deviation[0:n, layer, 0:1]).then_inc(norm_step, 1)
                dve.wait_ge(norm_step, count + 3)
                nc.vector.tensor_scalar(to[0:n, :], s[0:n, :], moments[0:n, layer, 0:1], deviation[0:n, layer, 1:2],
                                        ALU.subtract, ALU.mult).then_inc(semaphore, 1)

            def residual_0(b, n):
                dve.wait_ge(x_loaded, 16 * b + 16)
                dve.wait_ge(r0_ready, b + 1)
                nc.vector.tensor_tensor(s1[0:n, :], r0_ps[0:n, 0:D], x_sb[0:n, :], ALU.add
                                        ).then_inc(norm_step, 1)
                norm_moments(0, b, n, s1)

            def norm_0(b, n):
                normalise(0, b, n, s1, x1, x1_ready)

            def residual_1(b, n):
                dve.wait_ge(y_ready, b + 1)
                nc.vector.tensor_tensor(s2[0:n, :], y_ps[0:n, 0:D], x1[0:n, :], ALU.add).then_inc(norm_step, 1)
                norm_moments(1, b, n, s2)

            def norm_1(b, n):
                wait(dve, x2_stored, 16 * b)
                normalise(1, b, n, s2, x2, x2_ready)

            def pair(q, j, with_block):
                g, k = 2 * q, 2 * j
                make_onehots(g + 1, 1)
                if with_block is not None:
                    residual_0(with_block, P)
                add_sums(g, 0)
                stage_next(g, k)
                if with_block is not None:
                    norm_0(with_block, P)
                make_next_onehots(q)
                add_sums(g + 1, 1)
                stage_next(g + 1, k + 1)
                if with_block is not None:
                    residual_1(with_block, P)
                    norm_1(with_block, P)

            def stage_next(g, k):
                if not isinstance(g, int) or g + RING < FULL:
                    stage(g + RING, k)
                elif g + RING == FULL:
                    stage(FULL, 0, TAIL)

            def make_next_onehots(q):
                if isinstance(q, int) and q == NPAIR - 1:
                    make_onehots(FULL, 0, TAIL)
                else:
                    make_onehots(2 * q + 2, 0)

            dve.wait_ge(sums_zeroed, 1)
            make_onehots(0, 0)
            for j in range(PAIRS):
                pair(j, j, None)
            with dve.Fori(1, TURNS - 1) as t:
                for j in range(PAIRS):
                    go, b = block_turn(dve, t * PAIRS + j)
                    with dve.If(go > 0):
                        pair(t * PAIRS + j, j, b)
                    with dve.Else():
                        pair(t * PAIRS + j, j, None)
            for j in range(PAIRS):
                q = NPAIR - PAIRS + j
                go, b = block_turn(dve, q)
                with dve.If(go > 0):
                    pair(q, j, b)
                with dve.Else():
                    pair(q, j, None)
            add_sums(FULL, 0)
            dve.wait_ge(sums_added, NG)

            wide = dve.value_load(wide_i[0:1, 0:1], min_val=0, max_val=1)
            with dve.If(wide > 0):
                for n, lo, hi in ((P, 0, MAIN), (TAIL, MAIN, NG * SLOTS)):
                    ends_at = (local[0:n, lo:hi], dst_f[0:n, lo:hi])
                    step(nc.vector.tensor_scalar(ends_at[0], ends_at[0], float(WINDOW), None, ALU.is_ge))
                    step(nc.vector.tensor_scalar(ends_at[1], ends_at[1], 1.0, None, ALU.add))
                    step(nc.vector.tensor_tensor(ends_at[1], ends_at[1], ends_at[0], ALU.mult))
                    step(nc.vector.tensor_scalar(ends_at[1], ends_at[1], -1.0, None, ALU.add))

                def wide_group(g, n):
                    wait(dve, wide_summed, g * WINDOWS)
                    nc.vector.tensor_copy(staged[0:n, 0, :], src_sb[0:n, bass.ds(g * SLOTS, SLOTS)]
                                          ).then_inc(wide_staged, 1)
                    nc.vector.tensor_copy(relative[0:n, :], dst_f[0:n, bass.ds(g * SLOTS, SLOTS)]
                                          ).then_inc(wide_step, 1)
                    with dve.Fori(0, WINDOWS) as v:
                        turn = g * WINDOWS + v
                        dve.wait_ge(wide_step, turn + g + 1)
                        for s in range(SLOTS):
                            at = relative[0:n, s:s + 1]
                            nc.vector.tensor_scalar(wide_onehot[0:n, s, 1, :], iota[0:n, :], at, None, ALU.is_equal)
                            ins = nc.vector.tensor_scalar(wide_onehot[0:n, s, 0, :], iota[0:n, :], at,
                                                          weight_sb[0:n, bass.ds(g * SLOTS + s, 1)],
                                                          ALU.is_equal, ALU.mult)
                        ins.then_inc(wide_ready, 1)
                        dve.wait_ge(wide_ready, turn + 1)
                        nc.vector.tensor_scalar(relative[0:n, :], relative[0:n, :], float(-WIDE), None, ALU.add
                                                ).then_inc(wide_step, 1)
                        dve.wait_ge(wide_summed, turn + 1)
                        at = sums[:, :, bass.ds(v * WIDE, WIDE)]
                        nc.vector.tensor_tensor(at, at, group_ps[0][:, :, :], ALU.add).then_inc(wide_added, 1)
                        dve.wait_ge(wide_added, turn + 1)

                with dve.Fori(0, FULL) as g:
                    wide_group(g, P)
                wide_group(FULL, TAIL)
            nc.vector.memset(span[0:1, 0:1], 0.0).then_inc(sums_final, 1)

            def dense(b, n):
                residual_0(b, n)
                norm_0(b, n)
                residual_1(b, n)
                norm_1(b, n)

            remaining(dve, dense)

        @block.scalar
        def _(act):
            act.preload_act_table(ACT.Sqrt)
            act.wait_ge(zero_ready, 1)
            nc.scalar.activation(sums[:, :, :], zero[:, :].unsqueeze(2).to_broadcast([P, 2, SUMS]), ACT.Copy
                                 ).then_inc(sums_zeroed, 1)
            act.wait_ge(params_loaded, 16 * 6)
            act.wait_ge(consts_ready, 4)

            def relu_0(b, n):
                act.wait_ge(z0_ready, b + 1)
                nc.scalar.activation(r0T[:, 0:n], z0_ps[:, 0:n], ACT.Relu, bias=b0_sb[:, 0:1]
                                     ).then_inc(r0T_ready, 1)

            def deviate(layer, b, n):
                act.wait_ge(moments_ready, 2 * b + layer + 1)
                nc.scalar.activation(deviation[0:n, layer, 0:1], moments[0:n, layer, 1:2], ACT.Sqrt,
                                     bias=eps[0:n, :]).then_inc(deviation_ready, 1)

            def dense(b, n):
                relu_0(b, n)
                deviate(0, b, n)
                act.wait_ge(x1T_ready, b + 1)
                nc.scalar.activation(x1T[:, 0:n], x1T_ps[:, 0:n], ACT.Copy).then_inc(x1T_copied, 1)
                for k in range(HALVES):
                    act.wait_ge(h_ready, HALVES * b + k + 1)
                    nc.scalar.activation(hT[:, k, 0:n], h_ps[k][:, 0:n], ACT.Relu, bias=b1_sb[:, k:k + 1]
                                         ).then_inc(hT_ready, 1)
                deviate(1, b, n)
                act.wait_ge(x2_ready, b + 1)
                act.dma_start(out[bass.ds(b * P, n), :], x2[0:n, :]).then_inc(x2_stored, 16)

            act.wait_ge(tables_ready, 1)
            with act.Fori(PAIRS, NPAIR) as q:
                go, b = block_turn(act, q)
                with act.If(go > 0):
                    dense(b, P)
            remaining(act, dense)

        @block.tensor
        def _(pe):
            last = CH - 1
            pe.wait_ge(consts_ready, 4)
            for k in range(2):
                pe.wait_ge(ends_ready, k + 1)
                wait(pe, ends_reduced, k)
                for c in range(CH):
                    n = P if c < last else LASTCH
                    ins = nc.tensor.transpose(ends_ps[0:n, c * P:(c + 1) * P], ends[:, k, c * P:c * P + n],
                                              ident[:, :])
                ins.then_inc(ends_transposed, 1)
            for k, to in enumerate((z0_ps, r0_ps)):
                pe.wait_ge(ends_reduced, k + 1)
                for c in range(CH):
                    n = P if c < last else LASTCH
                    ins = nc.tensor.matmul(to[:, c * P:c * P + n], ones[0:n, :], diag[0:n, k, c, 0:n],
                                           start=True, stop=True)
                ins.then_inc(ends_spread, 1)

            def product(g, slot, kind, data, slots, n=P):
                for s in slots:
                    ins = nc.tensor.matmul(group_ps[slot][:, kind, 0:WINDOW], data[0:n, s, :],
                                           onehot[0:n, slot, s, kind, :], start=(s == 0), stop=(s == SLOTS - 1))
                return ins

            def z0(b, n):
                ins = nc.tensor.matmul(z0_ps[:, 0:n], w0_sb[:, :], sums[:, 0, bass.ds(b * P, n)],
                                       start=True, stop=True)
                ins.then_inc(z0_ready, 1)

            def r0(b, n):
                pe.wait_ge(r0T_ready, b + 1)
                nc.tensor.transpose(r0_ps[0:n, 0:D], r0T[:, 0:n], ident[:, :]).then_inc(r0_ready, 1)

            def x1_transposed(b, n):
                pe.wait_ge(x1_ready, b + 1)
                nc.tensor.transpose(x1T_ps[:, 0:n], x1[0:n, :], ident[0:n, 0:n]).then_inc(x1T_ready, 1)

            def hidden(b, n):
                pe.wait_ge(x1T_copied, b + 1)
                for k in range(HALVES):
                    nc.tensor.matmul(h_ps[k][:, 0:n], w1_sb[:, 1, k * P:(k + 1) * P], sums[:, 1, bass.ds(b * P, n)],
                                     start=True, stop=False)
                    nc.tensor.matmul(h_ps[k][:, 0:n], w1_sb[:, 0, k * P:(k + 1) * P], x1T[:, 0:n],
                                     start=False, stop=True).then_inc(h_ready, 1)

            def y(b, n):
                nc.tensor.matmul(y_ps[0:n, 0:D], ones[0:1, 0:n], b2_sb[0:1, :], start=True, stop=False)
                for k in range(HALVES):
                    pe.wait_ge(hT_ready, HALVES * b + k + 1)
                    ins = nc.tensor.matmul(y_ps[0:n, 0:D], hT[:, k, 0:n], w2_sb[:, k, :],
                                           start=False, stop=(k == HALVES - 1))
                ins.then_inc(y_ready, 1)

            def pair(q, t, j, b):
                g, k = 2 * q, 2 * j
                attrs = [attr_sb[:, j, a, :, :] for a in range(2)]
                if b is not None:
                    pe.wait_ge(sums_added, 2 * q - 1)
                    z0(b, P)
                wait(pe, sums_added, g - 1)
                pe.wait_ge(onehot_ready, g + 1)
                pe.wait_ge(attr_loaded[j], 16 * t + 16)
                product(g, 0, 1, attrs[0], range(SLOTS))
                if b is not None:
                    r0(b, P)
                pe.wait_ge(gathered[k], 16 * SLOTS * (t + 1))
                product(g, 0, 0, rows[:, k, :, :], range(SLOTS)).then_inc(group_summed, 1)
                wait(pe, sums_added, g)
                pe.wait_ge(onehot_ready, g + 2)
                product(g + 1, 1, 1, attrs[1], range(SLOTS))
                if b is not None:
                    x1_transposed(b, P)
                pe.wait_ge(gathered[k + 1], 16 * SLOTS * (t + 1))
                product(g + 1, 1, 0, rows[:, k + 1, :, :], range(0, 2))
                if b is not None:
                    hidden(b, P)
                product(g + 1, 1, 0, rows[:, k + 1, :, :], range(2, SLOTS)).then_inc(group_summed, 1)
                if b is not None:
                    y(b, P)

            for j in range(PAIRS):
                pair(j, 0, j, None)
            pe.wait_ge(tables_ready, 1)
            pe.wait_ge(params_loaded, 16 * 6)
            with pe.Fori(1, TURNS) as t:
                for j in range(PAIRS):
                    go, b = block_turn(pe, t * PAIRS + j)
                    with pe.If(go > 0):
                        pair(t * PAIRS + j, t, j, b)
                    with pe.Else():
                        pair(t * PAIRS + j, t, j, None)
            pe.wait_ge(sums_added, FULL - 1)
            pe.wait_ge(onehot_ready, NG)
            pe.wait_ge(attr_loaded[0], 16 * (TURNS + 1))
            product(FULL, 0, 1, attr_sb[:, 0, 0, :, :], range(SLOTS), TAIL)
            pe.wait_ge(gathered[0], 16 * SLOTS * (TURNS + 1))
            product(FULL, 0, 0, rows[:, 0, :, :], range(SLOTS), TAIL).then_inc(group_summed, 1)

            wide = pe.value_load(wide_i[0:1, 0:1], min_val=0, max_val=1)
            with pe.If(wide > 0):
                def wide_group(g, n):
                    pe.wait_ge(wide_attr_loaded, 16 * g + 16)
                    wait_apart(pe, wide_gathered, 16 * SLOTS * g + 16 * SLOTS, pe_waited)
                    with pe.Fori(0, WINDOWS) as v:
                        pe.wait_ge(wide_ready, g * WINDOWS + v + 1)
                        pe.wait_ge(wide_added, g * WINDOWS + v)
                        for kind, data in ((1, attr_sb[0:n, 0, 0, :, :]), (0, rows[0:n, 0, :, :])):
                            for s in range(SLOTS):
                                ins = nc.tensor.matmul(group_ps[0][:, kind, :], data[:, s, :],
                                                       wide_onehot[0:n, s, kind, :],
                                                       start=(s == 0), stop=(s == SLOTS - 1))
                        ins.then_inc(wide_summed, 1)

                with pe.Fori(0, FULL) as g:
                    wide_group(g, P)
                wide_group(FULL, TAIL)

            def dense(b, n):
                z0(b, n)
                r0(b, n)
                x1_transposed(b, n)
                hidden(b, n)
                y(b, n)

            pe.wait_ge(sums_final, 1)
            remaining(pe, dense)


def layout(x, src, dst, edge_attr_128, edge_weight, L0_gnn_w, L0_gnn_b, L1_gnn_W1, L1_gnn_b1, L1_gnn_W2, L1_gnn_b2):
    def by_group(a):
        full = a.shape[0] // GROUP
        whole = a[:full * GROUP].reshape(full, P, SLOTS).transpose(1, 0, 2).reshape(P, full * SLOTS)
        return whole, a[full * GROUP:].reshape(-1, SLOTS)

    named = {"x": x}
    for name, a in (("src", src), ("dst", dst), ("weight", edge_weight)):
        named[name], named[f"{name}_tail"] = by_group(a)
    named["attr"] = edge_attr_128
    named["w0"] = L0_gnn_w
    named["b0"] = L0_gnn_b.reshape(-1, 1)
    hid, both = L1_gnn_W1.shape
    named["w1"] = L1_gnn_W1.T.reshape(2, both // 2, hid).transpose(1, 0, 2)
    named["b1"] = L1_gnn_b1.reshape(-1, P).T
    named["w2"] = L1_gnn_W2.T.reshape(-1, P, L1_gnn_W2.shape[0]).transpose(1, 0, 2)
    named["b2"] = L1_gnn_b2.reshape(1, -1)
    return {k: np.ascontiguousarray(v) for k, v in named.items()}


def kernel(x, src, dst, edge_attr_128, edge_weight, L0_gnn_w, L0_gnn_b, L1_gnn_u, L1_gnn_W1, L1_gnn_b1,
           L1_gnn_W2, L1_gnn_b2):
    import concourse.bacc as bacc
    from concourse.bass_utils import run_bass_kernel_spmd

    arrays = layout(*(np.asarray(a) for a in (x, src, dst, edge_attr_128, edge_weight, L0_gnn_w, L0_gnn_b,
                                              L1_gnn_W1, L1_gnn_b1, L1_gnn_W2, L1_gnn_b2)))
    nc = bacc.Bacc("TRN2", target_bir_lowering=False, num_devices=1)
    args = {name: nc.dram_tensor(f"in_{name}_dram", a.shape, mybir.dt.from_np(a.dtype), kind="ExternalInput").ap()
            for name, a in arrays.items()}
    args["out"] = nc.dram_tensor("out_dram", x.shape, F32, kind="ExternalOutput").ap()
    build(nc, **args)
    r = run_bass_kernel_spmd(nc, [{f"in_{k}_dram": v for k, v in arrays.items()}], core_ids=[0])
    return r.results[0]["out_dram"]
```

```python
from contextlib import ExitStack

import numpy as np

import concourse.bass as bass
from concourse import mybir

F32 = mybir.dt.float32
I32 = mybir.dt.int32
ALU = mybir.AluOpType
ACT = mybir.ActivationFunctionType
AX = mybir.AxisListType

P = 128
SLOTS = 4
GROUP = P * SLOTS
WINDOW = 128
WIDE = 256
RING = 6
PAIRS = RING // 2
UNIT = 3
EPS = 1e-5


def wait(engine, semaphore, count):
    if not isinstance(count, int) or count > 0:
        engine.wait_ge(semaphore, count)


def wait_apart(engine, semaphore, count, waited):
    engine.wait_ge(semaphore, count)
    engine.sem_inc(waited, 1)


def build(nc, x, src, src_tail, dst, dst_tail, weight, weight_tail, attr, w0, b0, w1, b1, w2, b2, out):
    N, D = x.shape
    E = attr.shape[0]
    HID = b1.shape[0] * b1.shape[1]
    HALVES = HID // P
    assert D == P and HALVES == 2
    FULL = E // GROUP
    TAIL = (E - FULL * GROUP) // SLOTS
    NG = FULL + 1
    TURNS = FULL // RING
    assert FULL % RING == 0 and 0 < TAIL < P and TAIL * SLOTS + FULL * GROUP == E and NG <= 512
    SPAN = UNIT * P
    UNITS = N // SPAN
    LAST = N - UNITS * SPAN
    assert 0 < LAST < SPAN
    WHOLE = [P] * UNIT
    REST = [P] * (LAST // P) + [LAST % P] * (LAST % P > 0)
    WINDOWS = -(-N // WIDE)
    SUMS = max(WINDOWS * WIDE, N - 1 + WINDOW)
    SUMS += SUMS % 2
    CH = -(-NG // P)
    LASTCH = NG - (CH - 1) * P

    ctx = ExitStack()
    with ctx:
        def sbuf(name, shape, dtype=F32):
            return ctx.enter_context(nc.sbuf_tensor(name, shape, dtype))

        def psum(name, shape):
            return ctx.enter_context(nc.psum_tensor(name, shape, F32))

        def sem(name):
            return ctx.enter_context(nc.semaphore(name))

        sums = sbuf("sums", [P, 2, SUMS])
        src_sb = sbuf("src_sb", [P, NG * SLOTS], I32)
        dst_i = sbuf("dst_i", [P, NG * SLOTS], I32)
        dst_f = sbuf("dst_f", [P, NG * SLOTS])
        local = sbuf("local", [P, NG * SLOTS])
        weight_sb = sbuf("weight_sb", [P, NG * SLOTS])
        attr_sb = sbuf("attr_sb", [P, PAIRS, 2, SLOTS, D])
        rows = sbuf("rows", [P, RING, SLOTS, D])
        staged = sbuf("staged", [P, RING, SLOTS], I32)
        onehot = sbuf("onehot", [P, 2, 2, SLOTS, WINDOW])
        wide_onehot = onehot[:, :, :, :, :].rearrange("p a k s w -> p (a k s w)").rearrange(
            "p (s k w) -> p s k w", s=SLOTS, k=2)
        ident = sbuf("ident", [P, P])
        ones = sbuf("ones", [P, P])
        zero = sbuf("zero", [P, 512])
        eps = sbuf("eps", [P, 1])
        iota_i = sbuf("iota_i", [P, WIDE], I32)
        iota = sbuf("iota", [P, WIDE])
        w0_sb = sbuf("w0_sb", [P, D])
        b0_sb = sbuf("b0_sb", [P, 1])
        w1_sb = sbuf("w1_sb", [P, 2, HID])
        b1_sb = sbuf("b1_sb", [P, HALVES])
        w2_sb = sbuf("w2_sb", [P, HALVES, D])
        b2_sb = sbuf("b2_sb", [1, D])
        ends = sbuf("ends", [P, 2, NG])
        ends_t = sbuf("ends_t", [P, 2, CH])
        diag = sbuf("diag", [P, 2, CH, P])
        base_f = sbuf("base_f", [P, NG])
        span = sbuf("span", [P, NG])
        any_wide = sbuf("any_wide", [P, 3])
        wide_i = sbuf("wide_i", [1, 1], I32)
        later = sbuf("later", [1, 2, NG])
        ready_i = sbuf("ready_i", [1, TURNS], I32)
        ready = sbuf("ready", [1, TURNS])
        done = sbuf("done", [1, TURNS + 1])
        turns_i = sbuf("turns_i", [1, TURNS + 1, 2], I32)
        base_i = sbuf("base_i", [1, TURNS + 1, RING], I32)
        relative = sbuf("relative", [P, SLOTS])
        x_sb = sbuf("x_sb", [P, UNIT, D])
        r0T = sbuf("r0T", [P, SPAN])
        s1 = sbuf("s1", [P, UNIT, D])
        x1 = sbuf("x1", [P, UNIT, D])
        x1T = sbuf("x1T", [P, SPAN])
        hT = sbuf("hT", [P, HALVES, SPAN])
        s2 = sbuf("s2", [P, UNIT, D])
        x2 = sbuf("x2", [P, UNIT, D])
        stats = sbuf("stats", [P, 2, UNIT, 6])
        moments = sbuf("moments", [P, 2, UNIT, 2])
        deviation = sbuf("deviation", [P, 2, 2, UNIT])

        group_ps = [psum(f"group_ps{i}", [P, 2, WIDE]) for i in range(2)]
        z0_ps = psum("z0_ps", [P, 512])
        r0_ps = psum("r0_ps", [P, 512])
        x1T_ps = psum("x1T_ps", [P, 512])
        h_ps = [psum(f"h_ps{k}", [P, 512]) for k in range(HALVES)]
        y_ps = psum("y_ps", [P, 512])
        ends_ps = y_ps

        src_loaded = sem("src_loaded")
        dst_loaded = sem("dst_loaded")
        weight_loaded = sem("weight_loaded")
        params_loaded = sem("params_loaded")
        attr_loaded = [sem(f"attr_loaded{i}") for i in range(PAIRS)]
        gathered = [sem(f"gathered{i}") for i in range(RING)]
        consts_zeroed = sem("consts_zeroed")
        consts_ready = sem("consts_ready")
        zero_ready = sem("zero_ready")
        sums_zeroed = sem("sums_zeroed")
        setup_step = sem("setup_step")
        ends_ready = sem("ends_ready")
        ends_transposed = sem("ends_transposed")
        ends_reduced = sem("ends_reduced")
        diag_ready = sem("diag_ready")
        ends_spread = sem("ends_spread")
        base_read = sem("base_read")
        tables_ready = sem("tables_ready")
        staged_ready = sem("staged_ready")
        onehot_ready = sem("onehot_ready")
        weighted_ready = sem("weighted_ready")
        group_summed = sem("group_summed")
        sums_added = sem("sums_added")
        sums_final = sem("sums_final")
        wide_attr_loaded = sem("wide_attr_loaded")
        wide_staged = sem("wide_staged")
        wide_gathered = sem("wide_gathered")
        wide_step = sem("wide_step")
        wide_ready = sem("wide_ready")
        wide_summed = sem("wide_summed")
        wide_added = sem("wide_added")
        x_loaded = sem("x_loaded")
        z0_ready = sem("z0_ready")
        r0T_ready = sem("r0T_ready")
        r0_ready = sem("r0_ready")
        norm_step = sem("norm_step")
        moments_ready = sem("moments_ready")
        deviation_ready = sem("deviation_ready")
        x1_ready = sem("x1_ready")
        x1T_ready = sem("x1T_ready")
        x1T_copied = sem("x1T_copied")
        h_ready = sem("h_ready")
        hT_ready = sem("hT_ready")
        y_ready = sem("y_ready")
        x2_ready = sem("x2_ready")
        x2_stored = sem("x2_stored")
        pool_waited = sem("pool_waited")
        dve_waited = sem("dve_waited")
        pe_waited = sem("pe_waited")
        act_waited = sem("act_waited")

        src_v = src_sb[:, :].rearrange("p (g s) -> p g s", s=SLOTS)
        dst_v = dst_f[:, :].rearrange("p (g s) -> p g s", s=SLOTS)
        local_v = local[:, :].rearrange("p (g s) -> p g s", s=SLOTS)
        attr_pairs = attr[0:FULL * GROUP, :].rearrange("(q a p s) d -> q p a (s d)", a=2, p=P, s=SLOTS)
        attr_groups = attr[0:FULL * GROUP, :].rearrange("(g p s) d -> g p (s d)", p=P, s=SLOTS)
        attr_tail = attr[FULL * GROUP:E, :].rearrange("(p s) d -> p (s d)", s=SLOTS)
        MAIN = FULL * SLOTS

        def by_block(ps):
            return ps[:, 0:SPAN].rearrange("p (c d) -> p c d", d=P)


        def unit_of(engine, t):
            go, u = nc.values_load_multi_w_load_instructions(
                turns_i[0:1, bass.ds(t, 1), :].rearrange("a b c -> a (b c)"), engines=[engine.engine],
                min_val=0, max_val=UNITS - 1)[1]
            return go, u

        def spans(sizes):
            full = sum(n == P for n in sizes)
            return [(P, 0, full)] * (full > 0) + [(sizes[-1], full, full + 1)] * (full < len(sizes))

        def remaining(engine, body):
            first = unit_of(engine, TURNS)[1]
            with engine.Fori(first, UNITS) as u:
                body(u, WHOLE)
            body(UNITS, REST)

        block = ctx.enter_context(nc.Block())

        @block.sync
        def _(sp):
            sp.dma_start(src_sb[:, 0:MAIN], src).then_inc(src_loaded, 16)
            sp.dma_start(src_sb[0:TAIL, MAIN:], src_tail).then_inc(src_loaded, 16)
            sp.dma_start(dst_i[:, 0:MAIN], dst).then_inc(dst_loaded, 16)
            sp.dma_start(dst_i[0:TAIL, MAIN:], dst_tail).then_inc(dst_loaded, 16)
            sp.dma_start(weight_sb[:, 0:MAIN], weight).then_inc(weight_loaded, 16)
            sp.dma_start(weight_sb[0:TAIL, MAIN:], weight_tail).then_inc(weight_loaded, 16)

            def load_attr(q, slot):
                sp.dma_start(attr_sb[:, slot, :, :, :].rearrange("p a s d -> p a (s d)"),
                             attr_pairs[bass.ds(q, 1), :, :, :].rearrange("q p a n -> (q p) a n")
                             if not isinstance(q, int) else attr_pairs[q]).then_inc(attr_loaded[slot], 16)

            for j in range(PAIRS):
                load_attr(j, j)
            for sb, dram in ((w0_sb[:, :], w0), (b0_sb[:, :], b0), (w1_sb[:, :, :], w1), (b1_sb[:, :], b1),
                             (w2_sb[:, :, :], w2), (b2_sb[:, :], b2)):
                sp.dma_start(sb, dram).then_inc(params_loaded, 16)

            def load_x(u, sizes):
                wait(sp, x1_ready, u)
                for k, (n, lo, hi) in enumerate(spans(sizes)):
                    sp.dma_start(x_sb[0:n, lo:hi, :],
                                 x[bass.ds(u * SPAN + lo * P, n * (hi - lo)), :].rearrange(
                                     "(c p) d -> p c d", p=n)).then_inc(x_loaded, 16)

            sp.wait_ge(tables_ready, 1)
            with sp.Fori(0, TURNS - 1) as t:
                go, u = unit_of(sp, t)
                with sp.If(go > 0):
                    load_x(u, WHOLE)
                for j in range(PAIRS):
                    q = t * PAIRS + j
                    sp.wait_ge(group_summed, 2 * q + 2)
                    load_attr(q + PAIRS, j)
            go, u = unit_of(sp, TURNS - 1)
            with sp.If(go > 0):
                load_x(u, WHOLE)
            sp.wait_ge(group_summed, FULL - RING + 2)
            sp.dma_start(attr_sb[0:TAIL, 0, 0, :, :].rearrange("p s d -> p (s d)"), attr_tail
                         ).then_inc(attr_loaded[0], 16)

            wide = sp.value_load(wide_i[0:1, 0:1], min_val=0, max_val=1)
            with sp.If(wide > 0):
                sp.wait_ge(group_summed, NG)
                with sp.Fori(0, FULL) as g:
                    sp.wait_ge(wide_summed, g * WINDOWS)
                    sp.dma_start(attr_sb[:, 0, 0, :, :].rearrange("p s d -> p (s d)"),
                                 attr_groups[bass.ds(g, 1), :, :].rearrange("g p n -> (g p) n")
                                 ).then_inc(wide_attr_loaded, 16)
                sp.wait_ge(wide_summed, FULL * WINDOWS)
                sp.dma_start(attr_sb[0:TAIL, 0, 0, :, :].rearrange("p s d -> p (s d)"),
                             attr_tail).then_inc(wide_attr_loaded, 16)

            remaining(sp, load_x)
            sp.wait_ge(x2_stored, 16 * (UNITS + len(spans(REST))))

        @block.gpsimd
        def _(pool):
            pool.memset(zero[:, :], 0.0).then_inc(zero_ready, 1)
            pool.memset(ident[:, :], 0.0).then_inc(consts_zeroed, 1)
            pool.memset(ones[:, :], 1.0).then_inc(consts_ready, 1)
            pool.memset(eps[:, :], EPS).then_inc(consts_ready, 1)
            pool.iota(iota_i[:, :], pattern=[[1, WIDE]], base=0, channel_multiplier=0).then_inc(consts_ready, 1)
            pool.wait_ge(consts_zeroed, 1)
            pool.affine_select(out=ident[:, :], in_=ident[:, :], compare_op=ALU.not_equal, fill=1.0, base=0,
                               pattern=[[-1, P]], channel_multiplier=1).then_inc(consts_ready, 1)

            def gather(slot, n, semaphore):
                for s in range(SLOTS):
                    pool.indirect_dma_start(rows[0:n, slot, s, :], None, x,
                                            bass.IndirectOffsetOnAxis(ap=staged[0:n, slot, s:s + 1], axis=0)
                                            ).then_inc(semaphore, 16)

            with pool.Fori(0, TURNS) as t:
                for k in range(RING):
                    wait_apart(pool, staged_ready, t * RING + k + 1, pool_waited)
                    gather(k, P, gathered[k])
            pool.wait_ge(staged_ready, NG)
            gather(0, TAIL, gathered[0])

            pool.wait_ge(tables_ready, 1)
            wide = pool.value_load(wide_i[0:1, 0:1], min_val=0, max_val=1)
            with pool.If(wide > 0):
                with pool.Fori(0, FULL) as g:
                    wait_apart(pool, wide_staged, g + 1, pool_waited)
                    gather(0, P, wide_gathered)
                pool.wait_ge(wide_staged, NG)
                gather(0, TAIL, wide_gathered)

        @block.vector
        def _(dve):
            steps = [0]

            def step(instruction):
                steps[0] += 1
                instruction.then_inc(setup_step, 1)
                dve.wait_ge(setup_step, steps[0])

            def stage(g, slot, n=P):
                nc.vector.tensor_copy(staged[0:n, slot, :], src_sb[0:n, bass.ds(g * SLOTS, SLOTS)]
                                      ).then_inc(staged_ready, 1)

            dve.wait_ge(zero_ready, 1)
            for lo in range(0, SUMS, 512):
                hi = min(lo + 512, SUMS)
                ins = nc.vector.tensor_copy(sums[:, 1, lo:hi], zero[:, 0:hi - lo])
            ins.then_inc(sums_zeroed, 1)
            dve.wait_ge(src_loaded, 32)
            for k in range(RING):
                stage(k, k)

            dve.wait_ge(dst_loaded, 32)
            nc.vector.tensor_copy(dst_f[:, 0:MAIN], dst_i[:, 0:MAIN])
            nc.vector.memset(ends[:, 0, FULL:NG], 3e4)
            nc.vector.memset(ends[:, 1, FULL:NG], -3e4)
            step(nc.vector.tensor_copy(dst_f[0:TAIL, MAIN:], dst_i[0:TAIL, MAIN:]))
            for k, op in enumerate((ALU.min, ALU.max)):
                nc.vector.tensor_reduce(ends[:, k, 0:FULL], dst_v[:, 0:FULL, :], axis=AX.X, op=op)
                nc.vector.tensor_reduce(ends[0:TAIL, k, FULL:NG], dst_v[0:TAIL, FULL:NG, :], axis=AX.X,
                                        op=op).then_inc(ends_ready, 1)
            dve.wait_ge(consts_ready, 4)
            nc.vector.tensor_copy(iota[:, :], iota_i[:, :])
            last = CH - 1
            for k, op in enumerate((ALU.min, ALU.max)):
                dve.wait_ge(ends_transposed, k + 1)
                view = ends_ps[:, :].rearrange("p (c e) -> p c e", e=P)
                if CH > 1:
                    nc.vector.tensor_reduce(ends_t[:, k, 0:last], view[:, 0:last, :], axis=AX.X, op=op)
                step(nc.vector.tensor_reduce(ends_t[0:LASTCH, k, last:CH], view[0:LASTCH, last:CH, :],
                                             axis=AX.X, op=op))
                for c in range(CH):
                    n = P if c < last else LASTCH
                    ins = nc.vector.tensor_scalar(diag[0:n, k, c, :], ident[0:n, :], ends_t[0:n, k, c:c + 1], None,
                                                  ALU.mult)
                ins.then_inc(ends_reduced, 1)
            dve.wait_ge(ends_spread, 1)
            step(nc.vector.tensor_copy(base_f[:, :], z0_ps[:, 0:NG]))
            for n, lo, hi in ((P, 0, FULL), (TAIL, FULL, NG)):
                nc.vector.tensor_tensor(local_v[0:n, lo:hi, :], dst_v[0:n, lo:hi, :],
                                        base_f[0:n, lo:hi].unsqueeze(2).to_broadcast([n, hi - lo, SLOTS]),
                                        ALU.subtract)
            nc.vector.tensor_copy(base_i[0:1, :, :].rearrange("a t k -> a (t k)")[:, 0:NG], base_f[0:1, :])
            dve.wait_ge(ends_spread, 2)
            step(nc.vector.tensor_tensor(span[:, :], r0_ps[:, 0:NG], base_f[:, :], ALU.subtract))
            step(nc.vector.tensor_reduce(any_wide[:, 0:1], span[:, :], axis=AX.X, op=ALU.max))
            step(nc.vector.tensor_scalar(any_wide[:, 1:2], any_wide[:, 0:1], float(WINDOW), None, ALU.is_ge))
            nc.vector.tensor_copy(wide_i[0:1, :], any_wide[0:1, 1:2])
            step(nc.vector.tensor_scalar(any_wide[:, 2:3], any_wide[:, 1:2], -1.0, 1.0, ALU.mult, ALU.add))
            step(nc.vector.tensor_copy(later[0:1, 0, :], base_f[0:1, :]))
            reach, k = 1, 0
            while reach < NG:
                nc.vector.tensor_copy(later[0:1, 1 - k, NG - reach:NG], later[0:1, k, NG - reach:NG])
                step(nc.vector.tensor_tensor(later[0:1, 1 - k, 0:NG - reach], later[0:1, k, 0:NG - reach],
                                             later[0:1, k, reach:NG], ALU.min))
                reach, k = 2 * reach, 1 - k
            blocks_i = ready_i[0:1, 1:TURNS]
            step(nc.vector.tensor_copy(blocks_i, later[0:1, k, RING - 1:RING * (TURNS - 1):RING]))
            step(nc.vector.tensor_single_scalar(blocks_i, blocks_i, P.bit_length() - 1, ALU.arith_shift_right))
            step(nc.vector.tensor_scalar(blocks_i, blocks_i, float((1 << 16) // UNIT + 1), None, ALU.mult))
            step(nc.vector.tensor_single_scalar(blocks_i, blocks_i, 16, ALU.arith_shift_right))
            step(nc.vector.tensor_copy(ready[0:1, 1:TURNS], blocks_i))
            step(nc.vector.tensor_scalar(ready[0:1, 1:TURNS], ready[0:1, 1:TURNS], any_wide[0:1, 2:3],
                                         float(UNITS - 1), ALU.mult, ALU.min))
            step(nc.vector.memset(ready[0:1, 0:1], 0.0))
            step(nc.vector.memset(done[0:1, 0:1], 0.0))
            step(nc.vector.tensor_tensor_scan(done[0:1, 1:TURNS + 1], ones[0:1, 0:TURNS], ready[0:1, :], 0.0,
                                              ALU.add, ALU.min))
            nc.vector.memset(turns_i[0:1, TURNS:TURNS + 1, 0:1], 0)
            nc.vector.tensor_copy(turns_i[0:1, :, 1:2].rearrange("a b c -> a (b c)"), done[0:1, :])
            nc.vector.tensor_tensor(turns_i[0:1, 0:TURNS, 0:1].rearrange("a b c -> a (b c)"),
                                    done[0:1, 1:TURNS + 1], done[0:1, 0:TURNS], ALU.subtract
                                    ).then_inc(tables_ready, 1)
            dve.wait_ge(tables_ready, 1)

            def make_onehots(g, slot, n=P):
                wait(dve, group_summed, g - 1)
                at = local[0:n, bass.ds(g * SLOTS, SLOTS)].unsqueeze(2).to_broadcast([n, SLOTS, WINDOW])
                nc.vector.tensor_tensor(onehot[0:n, slot, 1, :, :],
                                        iota[0:n, 0:WINDOW].unsqueeze(1).to_broadcast([n, SLOTS, WINDOW]), at,
                                        ALU.is_equal).then_inc(onehot_ready, 1)

            def add_sums(g, slot, base):
                at = sums[:, :, bass.ds(base, WINDOW)]
                wait(dve, sums_added, g)
                dve.wait_ge(group_summed, g + 1)
                nc.vector.tensor_tensor(at, at, group_ps[slot][:, :, 0:WINDOW], ALU.add).then_inc(sums_added, 1)

            def norm_moments(layer, u, sizes, s, sources):
                count = 6 * u + 3 * layer
                for n, lo, hi in spans(sizes):
                    ins = nc.vector.tensor_tensor(s[0:n, lo:hi, :], sources[0][0:n, lo:hi, :],
                                                  sources[1][0:n, lo:hi, :], ALU.add)
                ins.then_inc(norm_step, 1)
                dve.wait_ge(norm_step, count + 1)
                for c, n in enumerate(sizes):
                    ins = nc.vector.bn_stats(stats[0:n, layer, c, :], s[0:n, c, :])
                ins.then_inc(norm_step, 1)
                wait_apart(dve, norm_step, count + 2, dve_waited)
                for c, n in enumerate(sizes):
                    ins = nc.vector.bn_aggr(moments[0:n, layer, c, :], stats[0:n, layer, c, :])
                ins.then_inc(moments_ready, 1)

            def normalise(layer, u, sizes, s, to, semaphore):
                count = 6 * u + 3 * layer
                dve.wait_ge(deviation_ready, 2 * u + layer + 1)
                for n, lo, hi in spans(sizes):
                    ins = nc.vector.reciprocal(deviation[0:n, layer, 1, lo:hi], deviation[0:n, layer, 0, lo:hi])
                ins.then_inc(norm_step, 1)
                dve.wait_ge(norm_step, count + 3)
                for c, n in enumerate(sizes):
                    ins = nc.vector.tensor_scalar(to[0:n, c, :], s[0:n, c, :], moments[0:n, layer, c, 0:1],
                                                  deviation[0:n, layer, 1, c:c + 1], ALU.subtract, ALU.mult)
                ins.then_inc(semaphore, 1)

            def residual_0(u, sizes):
                dve.wait_ge(x_loaded, 16 * (u + len(spans(sizes))))
                dve.wait_ge(r0_ready, u + 1)
                norm_moments(0, u, sizes, s1, (by_block(r0_ps), x_sb))

            def norm_0(u, sizes):
                normalise(0, u, sizes, s1, x1, x1_ready)

            def residual_1(u, sizes):
                dve.wait_ge(y_ready, u + 1)
                norm_moments(1, u, sizes, s2, (by_block(y_ps), x1))

            def norm_1(u, sizes):
                wait(dve, x2_stored, 16 * u)
                normalise(1, u, sizes, s2, x2, x2_ready)

            def turn(t, u):
                bases = nc.values_load_multi_w_load_instructions(
                    base_i[0:1, bass.ds(t, 1), :].rearrange("a b c -> a (b c)"), engines=[dve.engine],
                    min_val=0, max_val=N - 1)[1]
                for k in range(RING):
                    g = t * RING + k
                    if isinstance(g, int) and g + 1 == FULL:
                        make_onehots(FULL, 0, TAIL)
                    else:
                        make_onehots(g + 1, (k + 1) % 2)
                    if u is not None and k == 1:
                        residual_0(u, WHOLE)
                    if u is not None and k == RING - 1:
                        residual_1(u, WHOLE)
                    add_sums(g, k % 2, bases[k])
                    if not isinstance(g, int) or g + RING < FULL:
                        stage(g + RING, k)
                    elif g + RING == FULL:
                        stage(FULL, 0, TAIL)
                    if u is not None and k == 1:
                        norm_0(u, WHOLE)
                if u is not None:
                    norm_1(u, WHOLE)

            dve.wait_ge(sums_zeroed, 2)
            make_onehots(0, 0)
            turn(0, None)
            with dve.Fori(1, TURNS - 1) as t:
                go, u = unit_of(dve, t)
                with dve.If(go > 0):
                    turn(t, u)
                with dve.Else():
                    turn(t, None)
            go, u = unit_of(dve, TURNS - 1)
            with dve.If(go > 0):
                turn(TURNS - 1, u)
            with dve.Else():
                turn(TURNS - 1, None)
            add_sums(FULL, 0, dve.value_load(base_i[0:1, TURNS, 0:1], min_val=0, max_val=N - 1))
            dve.wait_ge(sums_added, NG)

            wide = dve.value_load(wide_i[0:1, 0:1], min_val=0, max_val=1)
            with dve.If(wide > 0):
                dve.wait_ge(weight_loaded, 32)
                for n, lo, hi in ((P, 0, MAIN), (TAIL, MAIN, NG * SLOTS)):
                    ends_at = (local[0:n, lo:hi], dst_f[0:n, lo:hi])
                    step(nc.vector.tensor_scalar(ends_at[0], ends_at[0], float(WINDOW), None, ALU.is_ge))
                    step(nc.vector.tensor_scalar(ends_at[1], ends_at[1], 1.0, None, ALU.add))
                    step(nc.vector.tensor_tensor(ends_at[1], ends_at[1], ends_at[0], ALU.mult))
                    step(nc.vector.tensor_scalar(ends_at[1], ends_at[1], -1.0, None, ALU.add))

                def wide_group(g, n):
                    wait(dve, wide_summed, g * WINDOWS)
                    nc.vector.tensor_copy(staged[0:n, 0, :], src_sb[0:n, bass.ds(g * SLOTS, SLOTS)]
                                          ).then_inc(wide_staged, 1)
                    nc.vector.tensor_copy(relative[0:n, :], dst_f[0:n, bass.ds(g * SLOTS, SLOTS)]
                                          ).then_inc(wide_step, 1)
                    with dve.Fori(0, WINDOWS) as v:
                        turn = g * WINDOWS + v
                        dve.wait_ge(wide_step, turn + g + 1)
                        for s in range(SLOTS):
                            at = relative[0:n, s:s + 1]
                            nc.vector.tensor_scalar(wide_onehot[0:n, s, 1, :], iota[0:n, :], at, None, ALU.is_equal)
                            ins = nc.vector.tensor_scalar(wide_onehot[0:n, s, 0, :], iota[0:n, :], at,
                                                          weight_sb[0:n, bass.ds(g * SLOTS + s, 1)],
                                                          ALU.is_equal, ALU.mult)
                        ins.then_inc(wide_ready, 1)
                        dve.wait_ge(wide_ready, turn + 1)
                        nc.vector.tensor_scalar(relative[0:n, :], relative[0:n, :], float(-WIDE), None, ALU.add
                                                ).then_inc(wide_step, 1)
                        dve.wait_ge(wide_summed, turn + 1)
                        at = sums[:, :, bass.ds(v * WIDE, WIDE)]
                        nc.vector.tensor_tensor(at, at, group_ps[0][:, :, :], ALU.add).then_inc(wide_added, 1)
                        dve.wait_ge(wide_added, turn + 1)

                with dve.Fori(0, FULL) as g:
                    wide_group(g, P)
                wide_group(FULL, TAIL)
            nc.vector.memset(span[0:1, 0:1], 0.0).then_inc(sums_final, 1)

            def dense(u, sizes):
                residual_0(u, sizes)
                norm_0(u, sizes)
                residual_1(u, sizes)
                norm_1(u, sizes)

            remaining(dve, dense)

        @block.scalar
        def _(act):
            act.preload_act_table(ACT.Sqrt)
            act.wait_ge(zero_ready, 1)
            nc.scalar.activation(sums[:, 0, :], zero[:, 0:1].to_broadcast([P, SUMS]), ACT.Copy
                                 ).then_inc(sums_zeroed, 1)
            act.wait_ge(weight_loaded, 32)

            def weigh(g, slot, n=P):
                wait_apart(act, onehot_ready, g + 1, act_waited)
                for s in range(SLOTS):
                    ins = nc.scalar.activation(onehot[0:n, slot, 0, s, :], onehot[0:n, slot, 1, s, :], ACT.Copy,
                                               scale=weight_sb[0:n, bass.ds(g * SLOTS + s, 1)])
                ins.then_inc(weighted_ready, 1)

            def relu_0(u, n):
                act.wait_ge(z0_ready, u + 1)
                nc.scalar.activation(r0T[:, 0:n], z0_ps[:, 0:n], ACT.Relu, bias=b0_sb[:, 0:1]
                                     ).then_inc(r0T_ready, 1)

            def deviate(layer, u, sizes):
                act.wait_ge(moments_ready, 2 * u + layer + 1)
                for n, lo, hi in spans(sizes):
                    ins = nc.scalar.activation(deviation[0:n, layer, 0, lo:hi], moments[0:n, layer, lo:hi, 1],
                                               ACT.Sqrt, bias=eps[0:n, :])
                ins.then_inc(deviation_ready, 1)

            def copy_x1T(u, n):
                act.wait_ge(x1T_ready, u + 1)
                nc.scalar.activation(x1T[:, 0:n], x1T_ps[:, 0:n], ACT.Copy).then_inc(x1T_copied, 1)

            def relu_1(u, n, k):
                act.wait_ge(h_ready, HALVES * u + k + 1)
                nc.scalar.activation(hT[:, k, 0:n], h_ps[k][:, 0:n], ACT.Relu, bias=b1_sb[:, k:k + 1]
                                     ).then_inc(hT_ready, 1)

            def store(u, sizes):
                act.wait_ge(x2_ready, u + 1)
                for n, lo, hi in spans(sizes):
                    act.dma_start(out[bass.ds(u * SPAN + lo * P, n * (hi - lo)), :].rearrange(
                        "(c p) d -> p c d", p=n), x2[0:n, lo:hi, :]).then_inc(x2_stored, 16)

            def turn(t, u):
                for k in range(RING):
                    g = t * RING + k
                    if isinstance(g, int) and g + 1 == FULL:
                        weigh(FULL, 0, TAIL)
                    else:
                        weigh(g + 1, (k + 1) % 2)
                    if u is None:
                        continue
                    if k == 0:
                        relu_0(u, SPAN)
                    if k == 1:
                        deviate(0, u, WHOLE)
                    if k == 2:
                        copy_x1T(u, SPAN)
                    if k in (3, 4):
                        relu_1(u, SPAN, k - 3)
                    if k == RING - 1:
                        deviate(1, u, WHOLE)
                        store(u, WHOLE)

            weigh(0, 0)
            turn(0, None)
            act.wait_ge(params_loaded, 16 * 6)
            act.wait_ge(tables_ready, 1)
            with act.Fori(1, TURNS - 1) as t:
                go, u = unit_of(act, t)
                with act.If(go > 0):
                    turn(t, u)
                with act.Else():
                    turn(t, None)
            go, u = unit_of(act, TURNS - 1)
            with act.If(go > 0):
                turn(TURNS - 1, u)
            with act.Else():
                turn(TURNS - 1, None)

            def dense(u, sizes):
                n = sum(sizes)
                relu_0(u, n)
                deviate(0, u, sizes)
                copy_x1T(u, n)
                relu_1(u, n, 0)
                relu_1(u, n, 1)
                deviate(1, u, sizes)
                store(u, sizes)

            remaining(act, dense)

        @block.tensor
        def _(pe):
            last = CH - 1
            pe.wait_ge(consts_ready, 4)
            for k in range(2):
                pe.wait_ge(ends_ready, k + 1)
                wait(pe, ends_reduced, k)
                for c in range(CH):
                    n = P if c < last else LASTCH
                    ins = nc.tensor.transpose(ends_ps[0:n, c * P:(c + 1) * P], ends[:, k, c * P:c * P + n],
                                              ident[:, :])
                ins.then_inc(ends_transposed, 1)
            for k, to in enumerate((z0_ps, r0_ps)):
                pe.wait_ge(ends_reduced, k + 1)
                for c in range(CH):
                    n = P if c < last else LASTCH
                    ins = nc.tensor.matmul(to[:, c * P:c * P + n], ones[0:n, :], diag[0:n, k, c, 0:n],
                                           start=True, stop=True)
                ins.then_inc(ends_spread, 1)

            def product(slot, kind, data, n=P):
                for s in range(SLOTS):
                    ins = nc.tensor.matmul(group_ps[slot][:, kind, 0:WINDOW], data[0:n, s, :],
                                           onehot[0:n, slot, kind, s, :], start=(s == 0), stop=(s == SLOTS - 1))
                return ins

            def z0(u, n):
                nc.tensor.matmul(z0_ps[:, 0:n], w0_sb[:, :], sums[:, 0, bass.ds(u * SPAN, n)],
                                 start=True, stop=True).then_inc(z0_ready, 1)

            def r0(u, sizes):
                pe.wait_ge(r0T_ready, u + 1)
                for c, n in enumerate(sizes):
                    ins = nc.tensor.transpose(r0_ps[0:n, c * P:(c + 1) * P], r0T[:, c * P:c * P + n], ident[:, :])
                ins.then_inc(r0_ready, 1)

            def x1_transposed(u, sizes):
                pe.wait_ge(x1_ready, u + 1)
                for c, n in enumerate(sizes):
                    ins = nc.tensor.transpose(x1T_ps[:, c * P:c * P + n], x1[0:n, c, :], ident[0:n, 0:n])
                ins.then_inc(x1T_ready, 1)

            def hidden(u, n, k):
                nc.tensor.matmul(h_ps[k][:, 0:n], w1_sb[:, 1, k * P:(k + 1) * P], sums[:, 1, bass.ds(u * SPAN, n)],
                                 start=True, stop=False)
                pe.wait_ge(x1T_copied, u + 1)
                nc.tensor.matmul(h_ps[k][:, 0:n], w1_sb[:, 0, k * P:(k + 1) * P], x1T[:, 0:n],
                                 start=False, stop=True).then_inc(h_ready, 1)

            def y(u, sizes):
                pe.wait_ge(hT_ready, HALVES * u + HALVES)
                for c, n in enumerate(sizes):
                    at = y_ps[0:n, c * P:(c + 1) * P]
                    nc.tensor.matmul(at, ones[0:1, 0:n], b2_sb[0:1, :], start=True, stop=False)
                    for k in range(HALVES):
                        ins = nc.tensor.matmul(at, hT[:, k, c * P:c * P + n], w2_sb[:, k, :],
                                               start=False, stop=(k == HALVES - 1))
                ins.then_inc(y_ready, 1)

            def turn(t, u):
                if u is not None:
                    pe.wait_ge(sums_added, t * RING - 1)
                    z0(u, SPAN)
                for k in range(RING):
                    g = t * RING + k
                    wait(pe, sums_added, g - 1)
                    pe.wait_ge(onehot_ready, g + 1)
                    if k % 2 == 0:
                        pe.wait_ge(attr_loaded[k // 2], 16 * t + 16)
                    product(k % 2, 1, attr_sb[:, k // 2, k % 2, :, :])
                    if u is not None:
                        if k == 1:
                            r0(u, WHOLE)
                        if k == 2:
                            x1_transposed(u, WHOLE)
                        if k in (3, 4):
                            hidden(u, SPAN, k - 3)
                        if k == RING - 1:
                            y(u, WHOLE)
                    pe.wait_ge(weighted_ready, g + 1)
                    pe.wait_ge(gathered[k], 16 * SLOTS * (t + 1))
                    product(k % 2, 0, rows[:, k, :, :]).then_inc(group_summed, 1)

            turn(0, None)
            pe.wait_ge(tables_ready, 1)
            pe.wait_ge(params_loaded, 16 * 6)
            with pe.Fori(1, TURNS) as t:
                go, u = unit_of(pe, t)
                with pe.If(go > 0):
                    turn(t, u)
                with pe.Else():
                    turn(t, None)
            pe.wait_ge(sums_added, FULL - 1)
            pe.wait_ge(onehot_ready, NG)
            pe.wait_ge(attr_loaded[0], 16 * (TURNS + 1))
            product(0, 1, attr_sb[:, 0, 0, :, :], TAIL)
            pe.wait_ge(weighted_ready, NG)
            pe.wait_ge(gathered[0], 16 * SLOTS * (TURNS + 1))
            product(0, 0, rows[:, 0, :, :], TAIL).then_inc(group_summed, 1)

            wide = pe.value_load(wide_i[0:1, 0:1], min_val=0, max_val=1)
            with pe.If(wide > 0):
                def wide_group(g, n):
                    pe.wait_ge(wide_attr_loaded, 16 * g + 16)
                    wait_apart(pe, wide_gathered, 16 * SLOTS * g + 16 * SLOTS, pe_waited)
                    with pe.Fori(0, WINDOWS) as v:
                        pe.wait_ge(wide_ready, g * WINDOWS + v + 1)
                        pe.wait_ge(wide_added, g * WINDOWS + v)
                        for kind, data in ((1, attr_sb[0:n, 0, 0, :, :]), (0, rows[0:n, 0, :, :])):
                            for s in range(SLOTS):
                                ins = nc.tensor.matmul(group_ps[0][:, kind, :], data[:, s, :],
                                                       wide_onehot[0:n, s, kind, :],
                                                       start=(s == 0), stop=(s == SLOTS - 1))
                        ins.then_inc(wide_summed, 1)

                with pe.Fori(0, FULL) as g:
                    wide_group(g, P)
                wide_group(FULL, TAIL)

            def dense(u, sizes):
                n = sum(sizes)
                z0(u, n)
                r0(u, sizes)
                x1_transposed(u, sizes)
                hidden(u, n, 0)
                hidden(u, n, 1)
                y(u, sizes)

            pe.wait_ge(sums_final, 1)
            remaining(pe, dense)


def layout(x, src, dst, edge_attr_128, edge_weight, L0_gnn_w, L0_gnn_b, L1_gnn_W1, L1_gnn_b1, L1_gnn_W2, L1_gnn_b2):
    def by_group(a):
        full = a.shape[0] // GROUP
        whole = a[:full * GROUP].reshape(full, P, SLOTS).transpose(1, 0, 2).reshape(P, full * SLOTS)
        return whole, a[full * GROUP:].reshape(-1, SLOTS)

    named = {"x": x}
    for name, a in (("src", src), ("dst", dst), ("weight", edge_weight)):
        named[name], named[f"{name}_tail"] = by_group(a)
    named["attr"] = edge_attr_128
    named["w0"] = L0_gnn_w
    named["b0"] = L0_gnn_b.reshape(-1, 1)
    hid, both = L1_gnn_W1.shape
    named["w1"] = L1_gnn_W1.T.reshape(2, both // 2, hid).transpose(1, 0, 2)
    named["b1"] = L1_gnn_b1.reshape(-1, P).T
    named["w2"] = L1_gnn_W2.T.reshape(-1, P, L1_gnn_W2.shape[0]).transpose(1, 0, 2)
    named["b2"] = L1_gnn_b2.reshape(1, -1)
    return {k: np.ascontiguousarray(v) for k, v in named.items()}


def kernel(x, src, dst, edge_attr_128, edge_weight, L0_gnn_w, L0_gnn_b, L1_gnn_u, L1_gnn_W1, L1_gnn_b1,
           L1_gnn_W2, L1_gnn_b2):
    import concourse.bacc as bacc
    from concourse.bass_utils import run_bass_kernel_spmd

    arrays = layout(*(np.asarray(a) for a in (x, src, dst, edge_attr_128, edge_weight, L0_gnn_w, L0_gnn_b,
                                              L1_gnn_W1, L1_gnn_b1, L1_gnn_W2, L1_gnn_b2)))
    nc = bacc.Bacc("TRN2", target_bir_lowering=False, num_devices=1)
    args = {name: nc.dram_tensor(f"in_{name}_dram", a.shape, mybir.dt.from_np(a.dtype), kind="ExternalInput").ap()
            for name, a in arrays.items()}
    args["out"] = nc.dram_tensor("out_dram", x.shape, F32, kind="ExternalOutput").ap()
    build(nc, **args)
    r = run_bass_kernel_spmd(nc, [{f"in_{k}_dram": v for k, v in arrays.items()}], core_ids=[0])
    return r.results[0]["out_dram"]
```

```python
from collections import namedtuple
from contextlib import ExitStack

import numpy as np

import concourse.bass as bass
from concourse import mybir

F32 = mybir.dt.float32
I32 = mybir.dt.int32
ALU = mybir.AluOpType
ACT = mybir.ActivationFunctionType
AX = mybir.AxisListType

P = 128
SLOTS = 4
GROUP = P * SLOTS
WINDOW = 128
WIDE = 256
RING = 6
PAIRS = RING // 2
UNIT = 3
ZEROES = 384
EPS = 1e-5

Part = namedtuple("Part", "before first sizes at bank last")


def wait(engine, semaphore, count):
    if not isinstance(count, int) or count > 0:
        engine.wait_ge(semaphore, count)


def wait_apart(engine, semaphore, count, waited):
    engine.wait_ge(semaphore, count)
    engine.sem_inc(waited, 1)


def build(nc, x, src, src_tail, dst, dst_tail, weight, weight_tail, attr, w0, b0, w1, b1, w2, b2, out):
    N, D = x.shape
    E = attr.shape[0]
    HID = b1.shape[0] * b1.shape[1]
    HALVES = HID // P
    assert D == P and HALVES == 2
    FULL = E // GROUP
    TAIL = (E - FULL * GROUP) // SLOTS
    NG = FULL + 1
    TURNS = FULL // RING
    assert FULL % RING == 0 and 0 < TAIL < P and TAIL * SLOTS + FULL * GROUP == E and NG <= 512
    SPAN = UNIT * P
    UNITS = N // SPAN
    FIRST_LAST = (UNITS - 1) * SPAN
    LAST_SIZES = [min(P, N - n) for n in range(FIRST_LAST, N, P)]
    LAST = len(LAST_SIZES)
    LASTS = [Part(UNITS - 1 + i, FIRST_LAST + i * P, [n], i, i % 2, True) for i, n in enumerate(LAST_SIZES)]
    assert N > UNITS * SPAN and LAST_SIZES[-1] < P
    WINDOWS = -(-N // WIDE)
    SUMS = max(WINDOWS * WIDE, N - 1 + WINDOW)
    SUMS += SUMS % 2
    ACT_ZEROES = SUMS // 4
    CH = -(-NG // P)
    LASTCH = NG - (CH - 1) * P

    ctx = ExitStack()
    with ctx:
        def sbuf(name, shape, dtype=F32):
            return ctx.enter_context(nc.sbuf_tensor(name, shape, dtype))

        def psum(name, shape):
            return ctx.enter_context(nc.psum_tensor(name, shape, F32))

        def sem(name):
            return ctx.enter_context(nc.semaphore(name))

        sums = sbuf("sums", [P, 2, SUMS])
        src_sb = sbuf("src_sb", [P, NG * SLOTS], I32)
        dst_i = sbuf("dst_i", [P, NG * SLOTS], I32)
        dst_f = sbuf("dst_f", [P, NG * SLOTS])
        local = sbuf("local", [P, NG * SLOTS])
        weight_sb = sbuf("weight_sb", [P, NG * SLOTS])
        attr_sb = sbuf("attr_sb", [P, PAIRS, 2, SLOTS, D])
        rows = sbuf("rows", [P, RING, SLOTS, D])
        staged = sbuf("staged", [P, RING, SLOTS], I32)
        onehot = sbuf("onehot", [P, 2, 2, SLOTS, WINDOW])
        wide_onehot = onehot[:, :, :, :, :].rearrange("p a k s w -> p (a k s w)").rearrange(
            "p (s k w) -> p s k w", s=SLOTS, k=2)
        ident = sbuf("ident", [P, P])
        ones = sbuf("ones", [P, P])
        zero = sbuf("zero", [P, ZEROES])
        eps = sbuf("eps", [P, 1])
        iota_i = sbuf("iota_i", [P, WIDE], I32)
        w0_sb = sbuf("w0_sb", [P, D])
        b0_sb = sbuf("b0_sb", [P, 1])
        w1_sb = sbuf("w1_sb", [P, 2, HID])
        b1_sb = sbuf("b1_sb", [P, HALVES])
        w2_sb = sbuf("w2_sb", [P, HALVES, D])
        b2_sb = sbuf("b2_sb", [1, D])
        ends = sbuf("ends", [P, 2, NG])
        ends_t = sbuf("ends_t", [P, 2, CH])
        diag = sbuf("diag", [P, 2, CH, P])
        base_f = sbuf("base_f", [P, NG])
        span = ends[:, 0, :]
        any_wide = sbuf("any_wide", [P, 3])
        wide_i = sbuf("wide_i", [1, 1], I32)
        later = sbuf("later", [1, 2, TURNS])
        ready_i = sbuf("ready_i", [1, TURNS], I32)
        ready = sbuf("ready", [1, TURNS])
        done = sbuf("done", [1, TURNS + 1])
        turns_i = sbuf("turns_i", [1, TURNS + 1, 2], I32)
        base_i = sbuf("base_i", [1, TURNS + 1, RING], I32)
        relative = sbuf("relative", [P, SLOTS])
        x_sb = sbuf("x_sb", [P, UNIT, D])
        x_last = sbuf("x_last", [P, LAST, D])
        r0T = sbuf("r0T", [P, LAST * P])
        s1 = sbuf("s1", [P, LAST, D])
        x1 = sbuf("x1", [P, LAST, D])
        x1T = sbuf("x1T", [P, LAST * P])
        hT = sbuf("hT", [P, HALVES, LAST * P])
        s2 = sbuf("s2", [P, LAST, D])
        x2 = sbuf("x2", [P, LAST, D])
        stats = sbuf("stats", [P, 2, LAST, 6])
        moments = sbuf("moments", [P, 2, LAST, 2])
        deviation = sbuf("deviation", [P, 2, 2, LAST])

        group_ps = [psum(f"group_ps{i}", [P, 2, WIDE]) for i in range(2)]
        z0_ps = [psum("z0_ps", [P, 512]), group_ps[0][:, :, :].rearrange("p a b -> p (a b)")]
        r0_ps = [psum("r0_ps", [P, 512]), group_ps[1][:, :, :].rearrange("p a b -> p (a b)")]
        x1T_ps = psum("x1T_ps", [P, 512])
        h_ps = psum("h_ps", [P, 512])
        iota = psum("iota", [P, 512])
        y_ps = psum("y_ps", [P, 512])
        ends_ps = y_ps

        first_staged = sem("first_staged")
        src_loaded = sem("src_loaded")
        dst_loaded = sem("dst_loaded")
        weight_loaded = sem("weight_loaded")
        params_loaded = sem("params_loaded")
        attr_loaded = [sem(f"attr_loaded{i}") for i in range(PAIRS)]
        gathered = [sem(f"gathered{i}") for i in range(RING)]
        consts_zeroed = sem("consts_zeroed")
        consts_ready = sem("consts_ready")
        zero_ready = sem("zero_ready")
        sums_zeroed = sem("sums_zeroed")
        setup_step = sem("setup_step")
        ends_ready = sem("ends_ready")
        ends_transposed = sem("ends_transposed")
        ends_reduced = sem("ends_reduced")
        diag_ready = sem("diag_ready")
        ends_spread = sem("ends_spread")
        base_read = sem("base_read")
        tables_ready = sem("tables_ready")
        staged_ready = sem("staged_ready")
        onehot_ready = sem("onehot_ready")
        weighted_ready = sem("weighted_ready")
        group_summed = sem("group_summed")
        sums_added = sem("sums_added")
        wide_attr_loaded = sem("wide_attr_loaded")
        wide_staged = sem("wide_staged")
        wide_gathered = sem("wide_gathered")
        wide_step = sem("wide_step")
        wide_ready = sem("wide_ready")
        wide_summed = sem("wide_summed")
        wide_added = sem("wide_added")
        x_loaded = sem("x_loaded")
        x_last_loaded = sem("x_last_loaded")
        z0_ready = sem("z0_ready")
        r0T_ready = sem("r0T_ready")
        r0_ready = sem("r0_ready")
        norm_step = [sem(f"norm_step{i}") for i in range(2)]
        moments_ready = [sem(f"moments_ready{i}") for i in range(2)]
        deviation_ready = [sem(f"deviation_ready{i}") for i in range(2)]
        x1_ready = sem("x1_ready")
        x1T_ready = sem("x1T_ready")
        x1T_copied = sem("x1T_copied")
        h_ready = sem("h_ready")
        hT_ready = sem("hT_ready")
        y_ready = sem("y_ready")
        x2_ready = sem("x2_ready")
        x2_stored = sem("x2_stored")
        pool_waited = sem("pool_waited")
        dve_waited = sem("dve_waited")
        pe_waited = sem("pe_waited")
        act_waited = sem("act_waited")

        src_v = src_sb[:, :].rearrange("p (g s) -> p g s", s=SLOTS)
        dst_v = dst_f[:, :].rearrange("p (g s) -> p g s", s=SLOTS)
        local_v = local[:, :].rearrange("p (g s) -> p g s", s=SLOTS)
        attr_pairs = attr[0:FULL * GROUP, :].rearrange("(q a p s) d -> q p a (s d)", a=2, p=P, s=SLOTS)
        attr_groups = attr[0:FULL * GROUP, :].rearrange("(g p s) d -> g p (s d)", p=P, s=SLOTS)
        attr_tail = attr[FULL * GROUP:E, :].rearrange("(p s) d -> p (s d)", s=SLOTS)
        MAIN = FULL * SLOTS

        def by_block(ps, part):
            return ps[:, 0:len(part.sizes) * P].rearrange("p (c d) -> p c d", d=P)

        def h_bank(part, k):
            return iota if part.last and k == 1 else h_ps

        def unit(u):
            return Part(u, u * SPAN, [P] * UNIT, 0, 0, False)

        def unit_of(engine, t):
            go, u = nc.values_load_multi_w_load_instructions(
                turns_i[0:1, bass.ds(t, 1), :].rearrange("a b c -> a (b c)"), engines=[engine.engine],
                min_val=0, max_val=UNITS - 1)[1]
            return go, u

        def remaining(engine, first, body):
            with engine.If(first < UNITS - 1):
                with engine.Fori(first, UNITS - 1) as u:
                    body(unit(u))

        block = ctx.enter_context(nc.Block())

        @block.sync
        def _(sp):
            sp.dma_start(staged[:, :, :].rearrange("p k s -> p (k s)"), src[:, 0:RING * SLOTS]
                         ).then_inc(first_staged, 16)
            sp.dma_start(dst_i[:, 0:MAIN], dst).then_inc(dst_loaded, 16)
            sp.dma_start(dst_i[0:TAIL, MAIN:], dst_tail).then_inc(dst_loaded, 16)
            sp.dma_start(weight_sb[:, 0:MAIN], weight).then_inc(weight_loaded, 16)
            sp.dma_start(weight_sb[0:TAIL, MAIN:], weight_tail).then_inc(weight_loaded, 16)

            def load_attr(q, slot):
                sp.dma_start(attr_sb[:, slot, :, :, :].rearrange("p a s d -> p a (s d)"),
                             attr_pairs[bass.ds(q, 1), :, :, :].rearrange("q p a n -> (q p) a n")
                             if not isinstance(q, int) else attr_pairs[q]).then_inc(attr_loaded[slot], 16)

            for j in range(PAIRS):
                load_attr(j, j)
            sp.dma_start(src_sb[:, 0:MAIN], src).then_inc(src_loaded, 16)
            sp.dma_start(src_sb[0:TAIL, MAIN:], src_tail).then_inc(src_loaded, 16)
            for sb, dram in ((w0_sb[:, :], w0), (b0_sb[:, :], b0), (w1_sb[:, :, :], w1), (b1_sb[:, :], b1),
                             (w2_sb[:, :, :], w2), (b2_sb[:, :], b2)):
                sp.dma_start(sb, dram).then_inc(params_loaded, 16)

            sp.dma_start(x_last[:, 0:LAST - 1, :], x[FIRST_LAST:FIRST_LAST + (LAST - 1) * P, :].rearrange(
                "(c p) d -> p c d", p=P)).then_inc(x_last_loaded, 16)
            sp.dma_start(x_last[0:LAST_SIZES[-1], LAST - 1, :], x[FIRST_LAST + (LAST - 1) * P:N, :]
                         ).then_inc(x_last_loaded, 16)

            def load_x(part):
                sp.wait_ge(x1_ready, part.before)
                sp.dma_start(x_sb[:, :, :], x[bass.ds(part.first, SPAN), :].rearrange("(c p) d -> p c d", p=P)
                             ).then_inc(x_loaded, 16)

            sp.wait_ge(tables_ready, 1)
            with sp.Fori(0, TURNS - 1) as t:
                go, u = unit_of(sp, t)
                with sp.If(go > 0):
                    load_x(unit(u))
                for j in range(PAIRS):
                    q = t * PAIRS + j
                    sp.wait_ge(group_summed, 2 * q + 2)
                    load_attr(q + PAIRS, j)
            go, u = unit_of(sp, TURNS - 1)
            with sp.If(go > 0):
                load_x(unit(u))
            sp.wait_ge(group_summed, FULL - RING + 2)
            sp.dma_start(attr_sb[0:TAIL, 0, 0, :, :].rearrange("p s d -> p (s d)"), attr_tail
                         ).then_inc(attr_loaded[0], 16)

            wide = sp.value_load(wide_i[0:1, 0:1], min_val=0, max_val=1)
            with sp.If(wide > 0):
                sp.wait_ge(group_summed, NG)
                with sp.Fori(0, FULL) as g:
                    sp.wait_ge(wide_summed, g * WINDOWS)
                    sp.dma_start(attr_sb[:, 0, 0, :, :].rearrange("p s d -> p (s d)"),
                                 attr_groups[bass.ds(g, 1), :, :].rearrange("g p n -> (g p) n")
                                 ).then_inc(wide_attr_loaded, 16)
                sp.wait_ge(wide_summed, FULL * WINDOWS)
                sp.dma_start(attr_sb[0:TAIL, 0, 0, :, :].rearrange("p s d -> p (s d)"),
                             attr_tail).then_inc(wide_attr_loaded, 16)

            remaining(sp, unit_of(sp, TURNS)[1], load_x)
            for part in LASTS:
                sp.wait_ge(x2_ready, part.before + 1)
                n = part.sizes[0]
                sp.dma_start(out[part.first:part.first + n, :], x2[0:n, part.at, :]).then_inc(x2_stored, 16)
            sp.wait_ge(x2_stored, 16 * (UNITS - 1 + LAST))

        @block.gpsimd
        def _(pool):
            pool.memset(zero[:, :], 0.0).then_inc(zero_ready, 1)
            pool.memset(ident[:, :], 0.0).then_inc(consts_zeroed, 1)
            pool.memset(ones[:, :], 1.0).then_inc(consts_ready, 1)
            pool.memset(eps[:, :], EPS).then_inc(consts_ready, 1)
            pool.iota(iota_i[:, :], pattern=[[1, WIDE]], base=0, channel_multiplier=0).then_inc(consts_ready, 1)
            pool.wait_ge(consts_zeroed, 1)
            pool.affine_select(out=ident[:, :], in_=ident[:, :], compare_op=ALU.not_equal, fill=1.0, base=0,
                               pattern=[[-1, P]], channel_multiplier=1).then_inc(consts_ready, 1)

            def gather(slot, n, semaphore):
                for s in range(SLOTS):
                    pool.indirect_dma_start(rows[0:n, slot, s, :], None, x,
                                            bass.IndirectOffsetOnAxis(ap=staged[0:n, slot, s:s + 1], axis=0)
                                            ).then_inc(semaphore, 16)

            pool.wait_ge(first_staged, 16)
            for k in range(RING):
                gather(k, P, gathered[k])
            with pool.Fori(1, TURNS) as t:
                for k in range(RING):
                    wait_apart(pool, staged_ready, (t - 1) * RING + k + 1, pool_waited)
                    gather(k, P, gathered[k])
            pool.wait_ge(staged_ready, NG - RING)
            gather(0, TAIL, gathered[0])

            pool.wait_ge(tables_ready, 1)
            wide = pool.value_load(wide_i[0:1, 0:1], min_val=0, max_val=1)
            with pool.If(wide > 0):
                with pool.Fori(0, FULL) as g:
                    wait_apart(pool, wide_staged, g + 1, pool_waited)
                    gather(0, P, wide_gathered)
                pool.wait_ge(wide_staged, NG)
                gather(0, TAIL, wide_gathered)

        @block.vector
        def _(dve):
            steps = [0]

            def step(instruction):
                steps[0] += 1
                instruction.then_inc(setup_step, 1)
                dve.wait_ge(setup_step, steps[0])

            def stage(g, slot, n=P):
                nc.vector.tensor_copy(staged[0:n, slot, :], src_sb[0:n, bass.ds(g * SLOTS, SLOTS)]
                                      ).then_inc(staged_ready, 1)

            dve.wait_ge(zero_ready, 1)
            for lo in range(ACT_ZEROES, SUMS, ZEROES):
                hi = min(lo + ZEROES, SUMS)
                ins = nc.vector.tensor_copy(sums[:, 1, lo:hi], zero[:, 0:hi - lo])
            ins.then_inc(sums_zeroed, 1)

            def make_onehots(g, slot, n=P):
                wait(dve, group_summed, g - 1)
                at = local[0:n, bass.ds(g * SLOTS, SLOTS)].unsqueeze(2).to_broadcast([n, SLOTS, WINDOW])
                nc.vector.tensor_tensor(onehot[0:n, slot, 1, :, :],
                                        iota[0:n, 0:WINDOW].unsqueeze(1).to_broadcast([n, SLOTS, WINDOW]), at,
                                        ALU.is_equal).then_inc(onehot_ready, 1)

            dve.wait_ge(dst_loaded, 32)
            nc.vector.tensor_copy(dst_f[:, 0:MAIN], dst_i[:, 0:MAIN])
            nc.vector.memset(ends[:, 0, FULL:NG], 3e4)
            nc.vector.memset(ends[:, 1, FULL:NG], -3e4)
            step(nc.vector.tensor_copy(dst_f[0:TAIL, MAIN:], dst_i[0:TAIL, MAIN:]))
            for k, op in enumerate((ALU.min, ALU.max)):
                nc.vector.tensor_reduce(ends[:, k, 0:FULL], dst_v[:, 0:FULL, :], axis=AX.X, op=op)
                nc.vector.tensor_reduce(ends[0:TAIL, k, FULL:NG], dst_v[0:TAIL, FULL:NG, :], axis=AX.X,
                                        op=op).then_inc(ends_ready, 1)
            dve.wait_ge(consts_ready, 4)
            nc.vector.tensor_copy(iota[:, 0:WIDE], iota_i[:, :])
            last = CH - 1
            for k, op in enumerate((ALU.min, ALU.max)):
                dve.wait_ge(ends_transposed, k + 1)
                view = ends_ps[:, :].rearrange("p (c e) -> p c e", e=P)
                if CH > 1:
                    nc.vector.tensor_reduce(ends_t[:, k, 0:last], view[:, 0:last, :], axis=AX.X, op=op)
                step(nc.vector.tensor_reduce(ends_t[0:LASTCH, k, last:CH], view[0:LASTCH, last:CH, :],
                                             axis=AX.X, op=op))
                for c in range(CH):
                    n = P if c < last else LASTCH
                    ins = nc.vector.tensor_scalar(diag[0:n, k, c, :], ident[0:n, :], ends_t[0:n, k, c:c + 1], None,
                                                  ALU.mult)
                ins.then_inc(ends_reduced, 1)
            dve.wait_ge(ends_spread, 1)
            step(nc.vector.tensor_copy(base_f[:, :], z0_ps[0][:, 0:NG]))
            nc.vector.tensor_copy(base_i[0:1, :, :].rearrange("a t k -> a (t k)")[:, 0:NG], base_f[0:1, :])
            for n, lo, hi in ((TAIL, FULL, NG), (P, 0, FULL)):
                ins = nc.vector.tensor_tensor(local_v[0:n, lo:hi, :], dst_v[0:n, lo:hi, :],
                                              base_f[0:n, lo:hi].unsqueeze(2).to_broadcast([n, hi - lo, SLOTS]),
                                              ALU.subtract)
            step(ins)
            make_onehots(0, 0)

            def make_tables():
                dve.wait_ge(ends_spread, 2)
                step(nc.vector.tensor_tensor(span, r0_ps[0][:, 0:NG], base_f[:, :], ALU.subtract))
                step(nc.vector.tensor_reduce(any_wide[:, 0:1], span, axis=AX.X, op=ALU.max))
                step(nc.vector.tensor_scalar(any_wide[:, 1:2], any_wide[:, 0:1], float(WINDOW), None, ALU.is_ge))
                nc.vector.tensor_copy(wide_i[0:1, :], any_wide[0:1, 1:2])
                step(nc.vector.tensor_scalar(any_wide[:, 2:3], any_wide[:, 1:2], -1.0, 1.0, ALU.mult, ALU.add))
                rest_of = NG - (RING * TURNS - 1)
                nc.vector.tensor_reduce(later[0:1, 0, 0:TURNS - 1],
                                        base_f[0:1, RING - 1:RING * TURNS - 1].rearrange("a (t k) -> a t k", k=RING),
                                        axis=AX.X, op=ALU.min)
                step(nc.vector.tensor_reduce(later[0:1, 0, TURNS - 1:TURNS], base_f[0:1, NG - rest_of:NG], axis=AX.X,
                                             op=ALU.min))
                reach, k = 1, 0
                while reach < TURNS:
                    nc.vector.tensor_copy(later[0:1, 1 - k, TURNS - reach:TURNS], later[0:1, k, TURNS - reach:TURNS])
                    step(nc.vector.tensor_tensor(later[0:1, 1 - k, 0:TURNS - reach], later[0:1, k, 0:TURNS - reach],
                                                 later[0:1, k, reach:TURNS], ALU.min))
                    reach, k = 2 * reach, 1 - k
                blocks_i = ready_i[0:1, 1:TURNS]
                step(nc.vector.tensor_copy(blocks_i, later[0:1, k, 0:TURNS - 1]))
                step(nc.vector.tensor_single_scalar(blocks_i, blocks_i, P.bit_length() - 1, ALU.arith_shift_right))
                step(nc.vector.tensor_scalar(blocks_i, blocks_i, float((1 << 16) // UNIT + 1), None, ALU.mult))
                step(nc.vector.tensor_single_scalar(blocks_i, blocks_i, 16, ALU.arith_shift_right))
                step(nc.vector.tensor_copy(ready[0:1, 1:TURNS], blocks_i))
                step(nc.vector.tensor_scalar(ready[0:1, 1:TURNS], ready[0:1, 1:TURNS], any_wide[0:1, 2:3],
                                             float(UNITS - 1), ALU.mult, ALU.min))
                step(nc.vector.memset(ready[0:1, 0:1], 0.0))
                step(nc.vector.memset(done[0:1, 0:1], 0.0))
                step(nc.vector.tensor_tensor_scan(done[0:1, 1:TURNS + 1], ones[0:1, 0:TURNS], ready[0:1, :], 0.0,
                                                  ALU.add, ALU.min))
                step(nc.vector.memset(turns_i[0:1, TURNS:TURNS + 1, 0:1], 0))
                nc.vector.tensor_copy(turns_i[0:1, :, 1:2].rearrange("a b c -> a (b c)"), done[0:1, :])
                nc.vector.tensor_tensor(turns_i[0:1, 0:TURNS, 0:1].rearrange("a b c -> a (b c)"),
                                        done[0:1, 1:TURNS + 1], done[0:1, 0:TURNS], ALU.subtract
                                        ).then_inc(tables_ready, 1)

            def add_sums(g, slot, base):
                at = sums[:, :, bass.ds(base, WINDOW)]
                wait(dve, sums_added, g)
                dve.wait_ge(group_summed, g + 1)
                nc.vector.tensor_tensor(at, at, group_ps[slot][:, :, 0:WINDOW], ALU.add).then_inc(sums_added, 1)

            def norm_moments(layer, part, s, sources):
                steps = norm_step[layer]
                n = part.sizes[0]
                at = slice(part.at, part.at + len(part.sizes))
                nc.vector.tensor_tensor(s[0:n, at, :], sources[0][0:n, :, :], sources[1][0:n, :, :], ALU.add
                                        ).then_inc(steps, 1)
                dve.wait_ge(steps, 3 * part.before + 1)
                for c in range(at.start, at.stop):
                    ins = nc.vector.bn_stats(stats[0:n, layer, c, :], s[0:n, c, :])
                ins.then_inc(steps, 1)
                wait_apart(dve, steps, 3 * part.before + 2, dve_waited)
                for c in range(at.start, at.stop):
                    ins = nc.vector.bn_aggr(moments[0:n, layer, c, :], stats[0:n, layer, c, :])
                ins.then_inc(moments_ready[layer], 1)

            def normalise(layer, part, s, to, semaphore):
                n = part.sizes[0]
                at = slice(part.at, part.at + len(part.sizes))
                dve.wait_ge(deviation_ready[layer], part.before + 1)
                nc.vector.reciprocal(deviation[0:n, layer, 1, at], deviation[0:n, layer, 0, at]
                                     ).then_inc(norm_step[layer], 1)
                dve.wait_ge(norm_step[layer], 3 * part.before + 3)
                for c in range(at.start, at.stop):
                    ins = nc.vector.tensor_scalar(to[0:n, c, :], s[0:n, c, :], moments[0:n, layer, c, 0:1],
                                                  deviation[0:n, layer, 1, c:c + 1], ALU.subtract, ALU.mult)
                ins.then_inc(semaphore, 1)

            def residual_0(part, own_x):
                dve.wait_ge(r0_ready, part.before + 1)
                norm_moments(0, part, s1, (by_block(r0_ps[part.bank], part), own_x))

            def norm_0(part):
                normalise(0, part, s1, x1, x1_ready)

            def residual_1(part):
                dve.wait_ge(y_ready, part.before + 1)
                norm_moments(1, part, s2, (by_block(y_ps, part), x1[:, part.at:part.at + len(part.sizes), :]))

            def norm_1(part):
                normalise(1, part, s2, x2, x2_ready)

            def turn(t, u):
                bases = nc.values_load_multi_w_load_instructions(
                    base_i[0:1, bass.ds(t, 1), :].rearrange("a b c -> a (b c)"), engines=[dve.engine],
                    min_val=0, max_val=N - 1)[1]
                for k in range(RING):
                    g = t * RING + k
                    if isinstance(g, int) and g + 1 == FULL:
                        make_onehots(FULL, 0, TAIL)
                    else:
                        make_onehots(g + 1, (k + 1) % 2)
                    if u is not None and k == 1:
                        dve.wait_ge(x_loaded, 16 * u + 16)
                        residual_0(unit(u), x_sb)
                    if u is not None and k == RING - 1:
                        residual_1(unit(u))
                    add_sums(g, k % 2, bases[k])
                    if not isinstance(g, int) or g + RING < FULL:
                        stage(g + RING, k)
                    elif g + RING == FULL:
                        stage(FULL, 0, TAIL)
                    if isinstance(t, int) and t == 0 and k == 0:
                        make_tables()
                    if u is not None and k == 1:
                        norm_0(unit(u))
                if u is not None:
                    dve.wait_ge(x2_stored, 16 * u)
                    norm_1(unit(u))

            dve.wait_ge(sums_zeroed, 2)
            dve.wait_ge(src_loaded, 32)
            turn(0, None)
            with dve.Fori(1, TURNS - 1) as t:
                go, u = unit_of(dve, t)
                with dve.If(go > 0):
                    turn(t, u)
                with dve.Else():
                    turn(t, None)
            go, u = unit_of(dve, TURNS - 1)
            with dve.If(go > 0):
                turn(TURNS - 1, u)
            with dve.Else():
                turn(TURNS - 1, None)
            last_base = dve.value_load(base_i[0:1, TURNS, 0:1], min_val=0, max_val=N - 1)
            wide = dve.value_load(wide_i[0:1, 0:1], min_val=0, max_val=1)
            first_left = unit_of(dve, TURNS)[1]
            add_sums(FULL, 0, last_base)
            dve.wait_ge(sums_added, NG)

            with dve.If(wide > 0):
                dve.wait_ge(weight_loaded, 32)
                for n, lo, hi in ((P, 0, MAIN), (TAIL, MAIN, NG * SLOTS)):
                    ends_at = (local[0:n, lo:hi], dst_f[0:n, lo:hi])
                    step(nc.vector.tensor_scalar(ends_at[0], ends_at[0], float(WINDOW), None, ALU.is_ge))
                    step(nc.vector.tensor_scalar(ends_at[1], ends_at[1], 1.0, None, ALU.add))
                    step(nc.vector.tensor_tensor(ends_at[1], ends_at[1], ends_at[0], ALU.mult))
                    step(nc.vector.tensor_scalar(ends_at[1], ends_at[1], -1.0, None, ALU.add))

                def wide_group(g, n):
                    wait(dve, wide_summed, g * WINDOWS)
                    nc.vector.tensor_copy(staged[0:n, 0, :], src_sb[0:n, bass.ds(g * SLOTS, SLOTS)]
                                          ).then_inc(wide_staged, 1)
                    nc.vector.tensor_copy(relative[0:n, :], dst_f[0:n, bass.ds(g * SLOTS, SLOTS)]
                                          ).then_inc(wide_step, 1)
                    with dve.Fori(0, WINDOWS) as v:
                        turn = g * WINDOWS + v
                        dve.wait_ge(wide_step, turn + g + 1)
                        for s in range(SLOTS):
                            at = relative[0:n, s:s + 1]
                            nc.vector.tensor_scalar(wide_onehot[0:n, s, 1, :], iota[0:n, 0:WIDE], at, None, ALU.is_equal)
                            ins = nc.vector.tensor_scalar(wide_onehot[0:n, s, 0, :], iota[0:n, 0:WIDE], at,
                                                          weight_sb[0:n, bass.ds(g * SLOTS + s, 1)],
                                                          ALU.is_equal, ALU.mult)
                        ins.then_inc(wide_ready, 1)
                        dve.wait_ge(wide_ready, turn + 1)
                        nc.vector.tensor_scalar(relative[0:n, :], relative[0:n, :], float(-WIDE), None, ALU.add
                                                ).then_inc(wide_step, 1)
                        dve.wait_ge(wide_summed, turn + 1)
                        at = sums[:, :, bass.ds(v * WIDE, WIDE)]
                        nc.vector.tensor_tensor(at, at, group_ps[0][:, :, :], ALU.add).then_inc(wide_added, 1)
                        dve.wait_ge(wide_added, turn + 1)

                with dve.Fori(0, FULL) as g:
                    wide_group(g, P)
                wide_group(FULL, TAIL)

            def dense(part):
                dve.wait_ge(x_loaded, 16 * part.before + 16)
                residual_0(part, x_sb)
                norm_0(part)
                residual_1(part)
                dve.wait_ge(x2_stored, 16 * part.before)
                norm_1(part)

            remaining(dve, first_left, dense)
            dve.wait_ge(x_last_loaded, 32)
            dve.wait_ge(x2_stored, 16 * (UNITS - 1))

            def last_0(i):
                residual_0(LASTS[i], x_last[:, i:i + 1, :])

            last_0(0)
            norm_0(LASTS[0])
            for i in range(LAST):
                if i + 1 < LAST:
                    last_0(i + 1)
                if i > 0:
                    norm_1(LASTS[i - 1])
                if i + 1 < LAST:
                    norm_0(LASTS[i + 1])
                residual_1(LASTS[i])
            norm_1(LASTS[-1])

        @block.scalar
        def _(act):
            act.preload_act_table(ACT.Sqrt)
            act.wait_ge(zero_ready, 1)
            nc.scalar.activation(sums[:, 0, :], zero[:, 0:1].to_broadcast([P, SUMS]), ACT.Copy)
            nc.scalar.activation(sums[:, 1, 0:ACT_ZEROES], zero[:, 0:1].to_broadcast([P, ACT_ZEROES]), ACT.Copy
                                 ).then_inc(sums_zeroed, 1)
            act.wait_ge(weight_loaded, 32)

            def weigh(g, slot, n=P):
                wait_apart(act, onehot_ready, g + 1, act_waited)
                for s in range(SLOTS):
                    ins = nc.scalar.activation(onehot[0:n, slot, 0, s, :], onehot[0:n, slot, 1, s, :], ACT.Copy,
                                               scale=weight_sb[0:n, bass.ds(g * SLOTS + s, 1)])
                ins.then_inc(weighted_ready, 1)

            def relu_0(part):
                n, at = sum(part.sizes), part.at * P
                act.wait_ge(z0_ready, part.before + 1)
                nc.scalar.activation(r0T[:, at:at + n], z0_ps[part.bank][:, 0:n], ACT.Relu, bias=b0_sb[:, 0:1]
                                     ).then_inc(r0T_ready, 1)

            def deviate(layer, part):
                n, at = part.sizes[0], slice(part.at, part.at + len(part.sizes))
                act.wait_ge(moments_ready[layer], part.before + 1)
                nc.scalar.activation(deviation[0:n, layer, 0, at], moments[0:n, layer, at, 1], ACT.Sqrt,
                                     bias=eps[0:n, :]).then_inc(deviation_ready[layer], 1)

            def copy_x1T(part):
                n, at = sum(part.sizes), part.at * P
                act.wait_ge(x1T_ready, part.before + 1)
                nc.scalar.activation(x1T[:, at:at + n], x1T_ps[:, 0:n], ACT.Copy).then_inc(x1T_copied, 1)

            def relu_1(part, k):
                n, at = sum(part.sizes), part.at * P
                act.wait_ge(h_ready, HALVES * part.before + k + 1)
                nc.scalar.activation(hT[:, k, at:at + n], h_bank(part, k)[:, 0:n], ACT.Relu, bias=b1_sb[:, k:k + 1]
                                     ).then_inc(hT_ready, 1)

            def store(part):
                act.wait_ge(x2_ready, part.before + 1)
                act.dma_start(out[bass.ds(part.first, SPAN), :].rearrange("(c p) d -> p c d", p=P),
                              x2[:, 0:UNIT, :]).then_inc(x2_stored, 16)

            def turn(t, u):
                for k in range(RING):
                    g = t * RING + k
                    if isinstance(g, int) and g + 1 == FULL:
                        weigh(FULL, 0, TAIL)
                    else:
                        weigh(g + 1, (k + 1) % 2)
                    if u is None:
                        continue
                    if k == 0:
                        relu_0(unit(u))
                    if k == 1:
                        deviate(0, unit(u))
                    if k == 2:
                        copy_x1T(unit(u))
                    if k in (3, 4):
                        relu_1(unit(u), k - 3)
                    if k == RING - 1:
                        deviate(1, unit(u))
                        store(unit(u))

            weigh(0, 0)
            turn(0, None)
            act.wait_ge(params_loaded, 16 * 6)
            act.wait_ge(tables_ready, 1)
            with act.Fori(1, TURNS - 1) as t:
                go, u = unit_of(act, t)
                with act.If(go > 0):
                    turn(t, u)
                with act.Else():
                    turn(t, None)
            go, u = unit_of(act, TURNS - 1)
            with act.If(go > 0):
                turn(TURNS - 1, u)
            with act.Else():
                turn(TURNS - 1, None)

            def dense(part):
                relu_0(part)
                deviate(0, part)
                copy_x1T(part)
                relu_1(part, 0)
                relu_1(part, 1)
                deviate(1, part)
                store(part)

            remaining(act, unit_of(act, TURNS)[1], dense)
            relu_0(LASTS[0])
            deviate(0, LASTS[0])
            relu_0(LASTS[1])
            for i in range(LAST):
                copy_x1T(LASTS[i])
                if i > 0:
                    deviate(1, LASTS[i - 1])
                if i + 1 < LAST:
                    deviate(0, LASTS[i + 1])
                relu_1(LASTS[i], 0)
                relu_1(LASTS[i], 1)
                if i + 2 < LAST:
                    relu_0(LASTS[i + 2])
            deviate(1, LASTS[-1])

        @block.tensor
        def _(pe):
            last = CH - 1
            pe.wait_ge(consts_ready, 4)
            for k in range(2):
                pe.wait_ge(ends_ready, k + 1)
                wait(pe, ends_reduced, k)
                for c in range(CH):
                    n = P if c < last else LASTCH
                    ins = nc.tensor.transpose(ends_ps[0:n, c * P:(c + 1) * P], ends[:, k, c * P:c * P + n],
                                              ident[:, :])
                ins.then_inc(ends_transposed, 1)
            for k, to in enumerate((z0_ps[0], r0_ps[0])):
                pe.wait_ge(ends_reduced, k + 1)
                for c in range(CH):
                    n = P if c < last else LASTCH
                    ins = nc.tensor.matmul(to[:, c * P:c * P + n], ones[0:n, :], diag[0:n, k, c, 0:n],
                                           start=True, stop=True)
                ins.then_inc(ends_spread, 1)

            def product(slot, kind, data, n=P):
                for s in range(SLOTS):
                    ins = nc.tensor.matmul(group_ps[slot][:, kind, 0:WINDOW], data[0:n, s, :],
                                           onehot[0:n, slot, kind, s, :], start=(s == 0), stop=(s == SLOTS - 1))
                return ins

            def z0(part):
                n = sum(part.sizes)
                nc.tensor.matmul(z0_ps[part.bank][:, 0:n], w0_sb[:, :], sums[:, 0, bass.ds(part.first, n)],
                                 start=True, stop=True).then_inc(z0_ready, 1)

            def r0(part):
                pe.wait_ge(r0T_ready, part.before + 1)
                for c, n in enumerate(part.sizes):
                    at = (part.at + c) * P
                    ins = nc.tensor.transpose(r0_ps[part.bank][0:n, c * P:(c + 1) * P], r0T[:, at:at + n],
                                              ident[:, :])
                ins.then_inc(r0_ready, 1)

            def x1_transposed(part):
                pe.wait_ge(x1_ready, part.before + 1)
                for c, n in enumerate(part.sizes):
                    ins = nc.tensor.transpose(x1T_ps[:, c * P:c * P + n], x1[0:n, part.at + c, :], ident[0:n, 0:n])
                ins.then_inc(x1T_ready, 1)

            def hidden(part, k):
                n, at = sum(part.sizes), part.at * P
                to = h_bank(part, k)[:, 0:n]
                if k == 1 and not part.last:
                    pe.wait_ge(hT_ready, HALVES * part.before + 1)
                nc.tensor.matmul(to, w1_sb[:, 1, k * P:(k + 1) * P],
                                 sums[:, 1, bass.ds(part.first, n)], start=True, stop=False)
                pe.wait_ge(x1T_copied, part.before + 1)
                nc.tensor.matmul(to, w1_sb[:, 0, k * P:(k + 1) * P], x1T[:, at:at + n],
                                 start=False, stop=True).then_inc(h_ready, 1)

            def y(part):
                pe.wait_ge(hT_ready, HALVES * part.before + HALVES)
                pe.wait_ge(moments_ready[1], part.before)
                for c, n in enumerate(part.sizes):
                    to = y_ps[0:n, c * P:(c + 1) * P]
                    at = (part.at + c) * P
                    nc.tensor.matmul(to, ones[0:1, 0:n], b2_sb[0:1, :], start=True, stop=False)
                    for k in range(HALVES):
                        ins = nc.tensor.matmul(to, hT[:, k, at:at + n], w2_sb[:, k, :],
                                               start=False, stop=(k == HALVES - 1))
                ins.then_inc(y_ready, 1)

            def turn(t, u):
                if u is not None:
                    pe.wait_ge(sums_added, t * RING - 1)
                    z0(unit(u))
                for k in range(RING):
                    g = t * RING + k
                    wait(pe, sums_added, g - 1)
                    pe.wait_ge(onehot_ready, g + 1)
                    if k % 2 == 0:
                        pe.wait_ge(attr_loaded[k // 2], 16 * t + 16)
                    product(k % 2, 1, attr_sb[:, k // 2, k % 2, :, :])
                    if u is not None:
                        if k == 1:
                            r0(unit(u))
                        if k == 2:
                            x1_transposed(unit(u))
                        if k in (3, 4):
                            hidden(unit(u), k - 3)
                        if k == RING - 1:
                            y(unit(u))
                    pe.wait_ge(weighted_ready, g + 1)
                    pe.wait_ge(gathered[k], 16 * SLOTS * (t + 1))
                    product(k % 2, 0, rows[:, k, :, :]).then_inc(group_summed, 1)

            turn(0, None)
            pe.wait_ge(tables_ready, 1)
            pe.wait_ge(params_loaded, 16 * 6)
            with pe.Fori(1, TURNS) as t:
                go, u = unit_of(pe, t)
                with pe.If(go > 0):
                    turn(t, u)
                with pe.Else():
                    turn(t, None)
            wide = pe.value_load(wide_i[0:1, 0:1], min_val=0, max_val=1)
            first_left = unit_of(pe, TURNS)[1]
            pe.wait_ge(sums_added, FULL - 1)
            pe.wait_ge(onehot_ready, NG)
            pe.wait_ge(attr_loaded[0], 16 * (TURNS + 1))
            product(0, 1, attr_sb[:, 0, 0, :, :], TAIL)
            pe.wait_ge(weighted_ready, NG)
            pe.wait_ge(gathered[0], 16 * SLOTS * (TURNS + 1))
            product(0, 0, rows[:, 0, :, :], TAIL).then_inc(group_summed, 1)

            with pe.If(wide > 0):
                def wide_group(g, n):
                    pe.wait_ge(wide_attr_loaded, 16 * g + 16)
                    wait_apart(pe, wide_gathered, 16 * SLOTS * g + 16 * SLOTS, pe_waited)
                    with pe.Fori(0, WINDOWS) as v:
                        pe.wait_ge(wide_ready, g * WINDOWS + v + 1)
                        pe.wait_ge(wide_added, g * WINDOWS + v)
                        for kind, data in ((1, attr_sb[0:n, 0, 0, :, :]), (0, rows[0:n, 0, :, :])):
                            for s in range(SLOTS):
                                ins = nc.tensor.matmul(group_ps[0][:, kind, :], data[:, s, :],
                                                       wide_onehot[0:n, s, kind, :],
                                                       start=(s == 0), stop=(s == SLOTS - 1))
                        ins.then_inc(wide_summed, 1)

                with pe.Fori(0, FULL) as g:
                    wide_group(g, P)
                wide_group(FULL, TAIL)
                wait_apart(pe, wide_added, NG * WINDOWS, pe_waited)

            def dense(part):
                z0(part)
                r0(part)
                x1_transposed(part)
                hidden(part, 0)
                hidden(part, 1)
                y(part)

            pe.wait_ge(sums_added, NG)
            remaining(pe, first_left, dense)
            z0(LASTS[0])
            z0(LASTS[1])
            r0(LASTS[0])
            for i in range(LAST):
                x1_transposed(LASTS[i])
                if i + 2 < LAST:
                    z0(LASTS[i + 2])
                if i + 1 < LAST:
                    r0(LASTS[i + 1])
                hidden(LASTS[i], 0)
                hidden(LASTS[i], 1)
                y(LASTS[i])


def layout(x, src, dst, edge_attr_128, edge_weight, L0_gnn_w, L0_gnn_b, L1_gnn_W1, L1_gnn_b1, L1_gnn_W2, L1_gnn_b2):
    def by_group(a):
        full = a.shape[0] // GROUP
        whole = a[:full * GROUP].reshape(full, P, SLOTS).transpose(1, 0, 2).reshape(P, full * SLOTS)
        return whole, a[full * GROUP:].reshape(-1, SLOTS)

    named = {"x": x}
    for name, a in (("src", src), ("dst", dst), ("weight", edge_weight)):
        named[name], named[f"{name}_tail"] = by_group(a)
    named["attr"] = edge_attr_128
    named["w0"] = L0_gnn_w
    named["b0"] = L0_gnn_b.reshape(-1, 1)
    hid, both = L1_gnn_W1.shape
    named["w1"] = L1_gnn_W1.T.reshape(2, both // 2, hid).transpose(1, 0, 2)
    named["b1"] = L1_gnn_b1.reshape(-1, P).T
    named["w2"] = L1_gnn_W2.T.reshape(-1, P, L1_gnn_W2.shape[0]).transpose(1, 0, 2)
    named["b2"] = L1_gnn_b2.reshape(1, -1)
    return {k: np.ascontiguousarray(v) for k, v in named.items()}


def kernel(x, src, dst, edge_attr_128, edge_weight, L0_gnn_w, L0_gnn_b, L1_gnn_u, L1_gnn_W1, L1_gnn_b1,
           L1_gnn_W2, L1_gnn_b2):
    import concourse.bacc as bacc
    from concourse.bass_utils import run_bass_kernel_spmd

    arrays = layout(*(np.asarray(a) for a in (x, src, dst, edge_attr_128, edge_weight, L0_gnn_w, L0_gnn_b,
                                              L1_gnn_W1, L1_gnn_b1, L1_gnn_W2, L1_gnn_b2)))
    nc = bacc.Bacc("TRN2", target_bir_lowering=False, num_devices=1)
    args = {name: nc.dram_tensor(f"in_{name}_dram", a.shape, mybir.dt.from_np(a.dtype), kind="ExternalInput").ap()
            for name, a in arrays.items()}
    args["out"] = nc.dram_tensor("out_dram", x.shape, F32, kind="ExternalOutput").ap()
    build(nc, **args)
    r = run_bass_kernel_spmd(nc, [{f"in_{k}_dram": v for k, v in arrays.items()}], core_ids=[0])
    return r.results[0]["out_dram"]
```
